# Optimizing a Trainium2 kernel written in Bass

```python
import numpy as np
import jax
import jax.numpy as jnp

def _softmax(x, axis=-1):
    return jax.nn.softmax(x, axis=axis)

def _gelu(x):
    return jax.nn.gelu(x, approximate=True)

def _silu(x):
    return jax.nn.silu(x)

def _sigmoid(x):
    return jax.nn.sigmoid(x)

def _layernorm(x, axis=-1, eps=1e-05):
    m = jnp.mean(x, axis=axis, keepdims=True)
    v = jnp.var(x, axis=axis, keepdims=True)
    return (x - m) / jnp.sqrt(v + eps)

def _scatter_add(tgt, idx, src, axis=0):
    return tgt.at[idx].add(src)

def _segment_sum(src, seg, n):
    return jax.ops.segment_sum(src, seg, n)
kernel_name = 'mk_gnn_preln_d1_gnn_r32_a22cc9'

def setup_inputs(seed: int=0):
    np.random.seed(seed)
    _w = jnp.asarray

    def _rec_inputs():
        import jax
        import jax.numpy as jnp
        _gk = jax.random.key(seed)
        x = -0.000202 + 1 * jax.random.normal(jax.random.fold_in(_gk, 1), (50000, 128), jnp.float32)
        src = jax.random.randint(jax.random.fold_in(_gk, 2), (25000,), 0, 50000, jnp.int32)
        dst = jnp.minimum((50000 * jax.random.uniform(jax.random.fold_in(_gk, 3), (25000,)) ** 2.0).astype(jnp.int32), 49999)
        _o = jnp.argsort(dst, stable=True)
        src = src[_o]
        dst = dst[_o]
        edge_weight = jax.random.uniform(jax.random.fold_in(_gk, 12), (25000,), jnp.float32, 0.0, 0.999998)
        return (x, src, dst, edge_weight)
    x, src, dst, edge_weight = _rec_inputs()

    def _L0_gnn_setup():
        import jax, jax.numpy as jnp
        import numpy as np
        N, E, H = (50000, 25000, 128)
        LN_EPS = 1e-05

        def layer_norm(x, gamma, beta):
            mu = jnp.mean(x, axis=-1, keepdims=True)
            var = jnp.mean((x - mu) ** 2, axis=-1, keepdims=True)
            return (x - mu) * jax.lax.rsqrt(var + LN_EPS) * gamma + beta
        key = jax.random.key(seed)
        ks = jax.random.split(key, 8)
        sc = 1.0 / np.sqrt(2 * H)
        return {'x': jax.random.normal(ks[0], (N, H), dtype=jnp.float32), 'edge_index': jax.random.randint(ks[1], (2, E), 0, N, dtype=jnp.int64), 'edge_weights': jax.random.uniform(ks[2], (E,), dtype=jnp.float32), 'msg_w': jax.random.normal(ks[3], (2 * H, H), dtype=jnp.float32) * sc, 'msg_b': jnp.zeros((H,), jnp.float32), 'msg_g': jnp.ones((H,), jnp.float32), 'msg_beta': jnp.zeros((H,), jnp.float32), 'upd_w': jax.random.normal(ks[4], (2 * H, H), dtype=jnp.float32) * sc, 'upd_b': jnp.zeros((H,), jnp.float32), 'upd_g': jnp.ones((H,), jnp.float32), 'upd_beta': jnp.zeros((H,), jnp.float32), 'gate_w': jax.random.normal(ks[5], (H, 1), dtype=jnp.float32) / np.sqrt(H), 'gate_b': jnp.zeros((1,), jnp.float32)}
    _L0_gnn_all = _L0_gnn_setup()
    _L0_gnn_in = {k: v for k, v in _L0_gnn_all.items() if k in ('msg_w', 'msg_b', 'msg_g', 'msg_beta', 'upd_w', 'upd_b', 'upd_g', 'upd_beta', 'gate_w', 'gate_b')}
    del _L0_gnn_all
    return {'x': x, 'src': src, 'dst': dst, 'edge_weight': edge_weight, 'L0_gnn_msg_w': _L0_gnn_in['msg_w'], 'L0_gnn_msg_b': _L0_gnn_in['msg_b'], 'L0_gnn_msg_g': _L0_gnn_in['msg_g'], 'L0_gnn_msg_beta': _L0_gnn_in['msg_beta'], 'L0_gnn_upd_w': _L0_gnn_in['upd_w'], 'L0_gnn_upd_b': _L0_gnn_in['upd_b'], 'L0_gnn_upd_g': _L0_gnn_in['upd_g'], 'L0_gnn_upd_beta': _L0_gnn_in['upd_beta'], 'L0_gnn_gate_w': _L0_gnn_in['gate_w'], 'L0_gnn_gate_b': _L0_gnn_in['gate_b']}

def reference(x, src, dst, edge_weight, L0_gnn_msg_w, L0_gnn_msg_b, L0_gnn_msg_g, L0_gnn_msg_beta, L0_gnn_upd_w, L0_gnn_upd_b, L0_gnn_upd_g, L0_gnn_upd_beta, L0_gnn_gate_w, L0_gnn_gate_b):
    import jax
    import jax.numpy as jnp

    def _L0_gnn_ref(x, edge_index, edge_weights, msg_w, msg_b, msg_g, msg_beta, upd_w, upd_b, upd_g, upd_beta, gate_w, gate_b):
        import jax, jax.numpy as jnp
        import numpy as np
        N, E, H = (50000, 25000, 128)
        LN_EPS = 1e-05

        def layer_norm(x, gamma, beta):
            mu = jnp.mean(x, axis=-1, keepdims=True)
            var = jnp.mean((x - mu) ** 2, axis=-1, keepdims=True)
            return (x - mu) * jax.lax.rsqrt(var + LN_EPS) * gamma + beta
        num_nodes = x.shape[0]
        src, dst = (edge_index[0], edge_index[1])
        em = jnp.concatenate([x[src], x[dst]], axis=-1)
        em = jax.nn.relu(layer_norm(em @ msg_w + msg_b, msg_g, msg_beta))
        em = em * edge_weights[:, None]
        msgs = jax.ops.segment_sum(em, dst, num_segments=num_nodes)
        counts = jax.ops.segment_sum(jnp.ones((src.shape[0], 1), x.dtype), dst, num_segments=num_nodes)
        valid = (counts > 0).astype(x.dtype)
        messages = msgs / (counts + 1e-08) * valid
        gate = jax.nn.sigmoid(x @ gate_w + gate_b)
        combined = jnp.concatenate([x, messages], axis=-1)
        h_new = jax.nn.relu(layer_norm(combined @ upd_w + upd_b, upd_g, upd_beta))
        return gate * h_new + (1.0 - gate) * x
    edge_index = jnp.stack([src, dst])
    h = jnp.maximum(_layernorm(x, axis=-1), 0.0)
    x = x + _L0_gnn_ref(h, edge_index, edge_weight, L0_gnn_msg_w, L0_gnn_msg_b, L0_gnn_msg_g, L0_gnn_msg_beta, L0_gnn_upd_w, L0_gnn_upd_b, L0_gnn_upd_g, L0_gnn_upd_beta, L0_gnn_gate_w, L0_gnn_gate_b)
    return x

_drawn_inputs = setup_inputs


def setup_inputs(seed=0):
    import zlib

    import numpy as np

    out = dict(_drawn_inputs(seed))
    spreads = {'L0_gnn_msg_b': (0.0, 0.659),
     'L0_gnn_msg_g': (1.0, 0.6),
     'L0_gnn_msg_beta': (0.0, 0.8),
     'L0_gnn_upd_b': (0.0, 0.1),
     'L0_gnn_upd_g': (1.0, 0.2),
     'L0_gnn_upd_beta': (0.0, 0.276)}
    factors = {}
    for name, (base, spread) in spreads.items():
        noise = np.random.default_rng([zlib.crc32(name.encode()), seed]).standard_normal(out[name].shape)
        drawn = base * np.exp(spread * noise) if base else spread * noise
        out[name] = jnp.asarray(drawn.astype(out[name].dtype))
    for name, factor in factors.items():
        out[name] = (out[name] * factor).astype(out[name].dtype)
    return out
```

```python
from contextlib import ExitStack

import concourse.bass as bass
from concourse import mybir

N, E, H = 50000, 25000, 128
P = 128
G = 4
NG = -(-N // (P * G))
LAST_BASE = N - P * G
J = 196
EG = J // G
EPAD = P * J
FULL = E // J
REST = E - FULL * J
RING = 32
EPS = 1e-5
FAR = float(1 << 20)
NO_NODE = 1 << 17
UN = 4

BORDERS1, VIOLATIONS, FLAG, BORDERS2, MATRICES, INDICES, WEIGHTS = 3, 7, 8, 10, 14, 26, 33

f32, bf16, i32 = mybir.dt.float32, mybir.dt.bfloat16, mybir.dt.int32
u32, u8 = mybir.dt.uint32, mybir.dt.uint8
ALU, ACT, AX = mybir.AluOpType, mybir.ActivationFunctionType, mybir.AxisListType


class Group:

    def __init__(self, at, turn=None):
        self.at, self.turn = at, turn

    def back(self, k):
        return Group(self.at - k, self.turn)

    def times(self, c, d=0):
        return c * self.at + d if self.turn is None else self.turn * (c * UN) + (c * self.at + d)

    def rounds(self, c, d=0):
        return c * (self.at // UN) + d if self.turn is None else self.turn * c + (c * (self.at // UN) + d)


class Steps:

    def __init__(self, sem, per):
        self.sem, self.per, self.eng, self.g, self.n = sem, per, None, None, 0

    def begin(self, eng, g):
        self.eng, self.g, self.n = eng, g, 0

    def mark(self, ins):
        self.n += 1
        assert self.n <= self.per
        ins.then_inc(self.sem, 1)

    def wait(self):
        self.eng.wait_ge(self.sem, self.g.times(self.per, self.n))

    def after(self, eng, g, n=None):
        eng.wait_ge(self.sem, g.times(self.per, self.per if n is None else n))


def run_steps(eng, step, n_groups, skew, lead):
    turns = (n_groups - lead) // UN
    stop = lead + turns * UN
    for s in range(lead):
        step(Group(s), True)
    with eng.Fori(0, turns) as i:
        for u in range(UN):
            step(Group(lead + u, i), False)
    for s in range(stop, n_groups + skew):
        step(Group(s), True)


def live(g, n_groups):
    return g.turn is not None or 0 <= g.at < n_groups


def build(nc, x, src, dst, edge_weight, msg_w, msg_b, msg_g, msg_beta, upd_w, upd_b, upd_g, upd_beta,
          gate_w, gate_b, out):
    ctx = ExitStack()
    nc.disable_value_cache = True
    with ctx:
        def sb(name, shape, dt=f32):
            return ctx.enter_context(nc.sbuf_tensor(name, shape, dt))

        def sem(name):
            return ctx.enter_context(nc.semaphore(name))

        def sem4(name):
            return [sem(f"{name}{i}") for i in range(4)]

        sums_dram = nc.dram_tensor("running_sums", (EPAD, H), f32).ap()
        sorted_dram = nc.dram_tensor("sorted_edges", (EPAD, 4), i32).ap()

        ring = sb("ring", [P, RING * 2 * G * H])
        xn = sb("xn", [P, 4 * G * H])
        ht = sb("ht", [P, 4, 2 * G * H])
        acc = sb("acc", [P, 4, G, H])
        at_ = sb("at", [P, 2, G * H])
        o = sb("o", [P, 4, G, H])
        xload = sb("xload", [P, 4, G, H])
        t_buf = sb("t_buf", [P, G, H])
        u_buf = sb("u_buf", [P, G, H])
        junk = sb("junk", [P, 2, G, H], bf16)
        junkm = sb("junkm", [P, 2, G, H], bf16)
        w_all = sb("w_all", [P, 4, H])
        w_u1 = sb("w_u1", [P, H + 1])
        g_msg = sb("g_msg", [P, H])
        be_msg = sb("be_msg", [P, H])
        g_upd = sb("g_upd", [P, H])
        be_upd = sb("be_upd", [P, H])
        ident = sb("ident", [P, P])
        ones = sb("ones", [P, P])
        below = sb("below", [P, P])
        above = sb("above", [P, P])
        bias = sb("bias", [1, 3, 2 * H + 1])
        bias_sum = sb("bias_sum", [1, 2])
        bias_b = sb("bias_b", [1, 3, 2 * H + 1], bf16)
        bias3 = sb("bias3", [3, 2 * H + 1], bf16)
        ones3 = sb("ones3", [3, P], bf16)
        wmean = sb("wmean", [P, 4])
        st = sb("st", [P, 4, 2 * G, 6])
        s_sum = sb("s_sum", [P, 2 * G])
        s_dif = sb("s_dif", [P, 2 * G])
        s_var = sb("s_var", [P, 2 * G])
        s_sq = sb("s_sq", [P, 2 * G])
        mu = sb("mu", [P, 4, 2 * G])
        var = sb("var", [P, 4, 2 * G])
        lnv = sb("lnv", [P, 4, 2 * G])
        rs = sb("rs", [P, 4, 2 * G])
        ss = sb("ss", [P, 2, G])
        ge = sb("ge", [P, 2, G])
        ln2 = sb("ln2", [P, 2, G])
        r2 = sb("r2", [P, 2, G])
        ssm = sb("ssm", [P, 2, G])
        lnm = sb("lnm", [P, 2, G])
        rm = sb("rm", [P, 2, G])
        e1 = sb("e1", [P, G])
        gt = sb("gt", [P, G])
        rg = sb("rg", [P, G])
        omg = sb("omg", [P, G])
        src_i = sb("src_i", [P, J], i32)
        dst_i = sb("dst_i", [P, J], i32)
        w_f = sb("w_f", [P, J])
        gidx = sb("gidx", [P, J], i32)
        sidx = sb("sidx", [P, J], i32)
        cont = sb("cont", [P, J + 1])
        wb = sb("wb", [P, J])
        carry_m = sb("carry_m", [P, P])
        tidx = sb("tidx", [P, 3], i32)
        flag_i = sb("flag_i", [1, 1], i32)
        eps_col = sb("eps_col", [P, 1])
        prep = acc[:, :, :, :].rearrange("p a b c -> p (a b c)")

        def pre(i, n=J):
            return prep[:, i * (J + 4):i * (J + 4) + n]

        dst_f, ones_j, run_f, run_b, is_first, is_last, cnt, ok, viol = (pre(i) for i in range(9))
        m2 = at_[:, 0, 0:P]
        dbf = at_[:, 0, P:2 * P]
        dbl = at_[:, 0, 2 * P:3 * P]
        scr = at_[:, 1, 0:P]
        col = at_[:, 1, P:P + 32]

        tail_x, tail_h, tail_f, tail_a = (xload[:, 0, k, :] for k in range(4))
        tail_o = xload[:, 1, 0, :]

        keys = ring[:, 0:EPAD]
        keys_i = keys.bitcast(i32)
        smaller = ring[:, EPAD:EPAD + EPAD // 8].bitcast(u8)
        spare = ring[:, EPAD + EPAD // 8:EPAD + EPAD // 8 + 5 * J + 8].bitcast(i32)
        rank_i = spare[:, 0:J]
        rec = spare[:, J:5 * J]
        stage_r, stage_e = spare[:, 5 * J:5 * J + 1], spare[:, 5 * J + 4:5 * J + 8]

        pt = ctx.enter_context(nc.psum_tensor("pt", [P, 2, G * H], f32))
        pm = ctx.enter_context(nc.psum_tensor("pm", [P, G, H], f32))
        pa = ctx.enter_context(nc.psum_tensor("pa", [P, G * H], f32))
        py = ctx.enter_context(nc.psum_tensor("py", [P, 2, G, 2 * H], f32))

        s_w = sem("weights_loaded")
        s_e = sem("edges_loaded")
        s_memset = sem("edge_pads_set")
        s_const = sem("constants_built")
        s_prep = sem("prep_done_by_vector")
        s_prep_pe = sem("prep_done_by_tensor")
        s_wready = sem("weights_centred")
        s_b3 = sem("bias_parts_placed")
        s_bsplit = sem("bias_parts_split")
        s_key = sem("sort_keys_loaded")
        s_rank = sem("edges_ranked")
        s_stage = sem("sort_row_staged")
        s_row = sem("sort_row_written")
        s_back = sem("sorted_edges_loaded")
        s_fall = sem("vector_steps_of_sort")
        s_x = sem4("x_loaded")
        s_st = sem4("node_rows_stored")
        s_gath = sem4("rows_gathered")
        s_scat = sem4("rows_scattered")
        s_sums = sem4("running_sums_stored")
        s_tx, s_tf, s_to = sem("tail_x_gathered"), sem("tail_sums_gathered"), sem("tail_scattered")

        def stages(kind):
            return {
                "stats": Steps(sem(f"{kind}_stats"), 4),
                "rstd": Steps(sem(f"{kind}_rstd"), 2),
                "norm": Steps(sem(f"{kind}_norm"), 2),
                "flip": Steps(sem(f"{kind}_flip"), 1),
                "ht": Steps(sem(f"{kind}_ht"), 1),
                "upd": Steps(sem(f"{kind}_upd"), 1),
                "post": Steps(sem(f"{kind}_post"), 3),
                "fin": Steps(sem(f"{kind}_fin"), 7),
            }

        nd, ed, tl = stages("node"), stages("edge"), stages("tail")
        for kind, d in (("edge", ed), ("tail", tl)):
            d["msg"] = Steps(sem(f"{kind}_msg"), 1)
            d["mstd"] = Steps(sem(f"{kind}_mstd"), 3)
            d["sum"] = Steps(sem(f"{kind}_sum"), 3 + G)
            d["aflip"] = Steps(sem(f"{kind}_aflip"), 1)
            d["at"] = Steps(sem(f"{kind}_at"), 1)

        def rows4(v):
            return v.rearrange("p (k h) -> p k h", h=H)

        def slot(g, part, base=None, n=G):
            if g.turn is None:
                a = (g.at % RING) * 2 * G * H + part * G * H
                return rows4(ring[:, a:a + n * H])
            return rows4(ring[:, bass.ds(base + part * G * H, n * H)])

        def slot_base(eng, g):
            return None if g.turn is None else eng.snap(((g.turn * UN + g.at) % RING) * (2 * G * H))

        def column(t, c, k):
            return t[:, c + k:c + k + 1] if isinstance(c, int) else t[:, bass.ds(c + k, 1)]

        def do_stats(dve, L, g, parts):
            L.begin(dve, g)
            s4 = g.at % 4
            k = 0
            for v in parts:
                for m in range(v.shape[1]):
                    last = nc.vector.bn_stats(st[:, s4, k, :], v[:, m, :])
                    k += 1
            L.mark(last)
            L.wait()
            a, b = st[:, s4, 0:k, 1], st[:, s4, 0:k, 4]
            nc.vector.tensor_tensor(s_sum[:, 0:k], a, b, ALU.add)
            nc.vector.tensor_tensor(s_dif[:, 0:k], a, b, ALU.subtract)
            L.mark(nc.vector.tensor_tensor(s_var[:, 0:k], st[:, s4, 0:k, 2], st[:, s4, 0:k, 5], ALU.add))
            L.wait()
            nc.vector.tensor_scalar(mu[:, s4, 0:k], s_sum[:, 0:k], 0.5, None, ALU.mult)
            L.mark(nc.vector.tensor_tensor(s_sq[:, 0:k], s_dif[:, 0:k], s_dif[:, 0:k], ALU.mult))
            L.wait()
            L.mark(nc.vector.scalar_tensor_tensor(var[:, s4, 0:k], s_sq[:, 0:k], H / 4, s_var[:, 0:k],
                                                  ALU.mult, ALU.add))

        def do_rstd(act, d, g, k):
            d["stats"].after(act, g)
            L = d["rstd"]
            L.begin(act, g)
            s4 = g.at % 4
            L.mark(nc.scalar.activation(lnv[:, s4, 0:k], var[:, s4, 0:k], ACT.Ln, bias=eps_col[:, :], scale=1.0 / H))
            L.wait()
            L.mark(nc.scalar.activation(rs[:, s4, 0:k], lnv[:, s4, 0:k], ACT.Exp, scale=-0.5))

        def normalise(g, dest, part, k0):
            for m in range(part.shape[1]):
                last = nc.vector.tensor_scalar(dest[:, k0 + m, :], part[:, m, :],
                                               mu[:, g.at % 4, k0 + m:k0 + m + 1],
                                               rs[:, g.at % 4, k0 + m:k0 + m + 1], ALU.subtract, ALU.mult)
            return last

        def do_post(act, d, g, n):
            d["upd"].after(act, g)
            L = d["post"]
            L.begin(act, g)
            b = g.at % 2
            for k in range(n):
                last = nc.scalar.activation(junk[:, b, k, :], py[:, b, k, 0:H], ACT.Square, accum_out=ss[:, b, k:k + 1])
            L.mark(last)
            nc.scalar.activation(ge[:, b, 0:n], py[:, b, 0:n, H], ACT.Exp, scale=-1.0)
            L.wait()
            L.mark(nc.scalar.activation(ln2[:, b, 0:n], ss[:, b, 0:n], ACT.Ln, bias=eps_col[:, :], scale=1.0 / H))
            L.wait()
            L.mark(nc.scalar.activation(r2[:, b, 0:n], ln2[:, b, 0:n], ACT.Exp, scale=-0.5))

        def do_fin(dve, d, g, h, xr, dest, n, before=None):
            d["post"].after(dve, g)
            L = d["fin"]
            L.begin(dve, g)
            b = g.at % 2
            L.mark(nc.vector.tensor_scalar(e1[:, 0:n], ge[:, b, 0:n], 1.0, None, ALU.add))
            L.wait()
            L.mark(nc.vector.reciprocal(gt[:, 0:n], e1[:, 0:n]))
            L.wait()
            nc.vector.tensor_tensor(rg[:, 0:n], r2[:, b, 0:n], gt[:, 0:n], ALU.mult)
            L.mark(nc.vector.tensor_scalar(omg[:, 0:n], gt[:, 0:n], -1.0, 1.0, ALU.mult, ALU.add))
            L.wait()
            for k in range(n):
                last = nc.vector.scalar_tensor_tensor(t_buf[:, k, :], py[:, b, k, 0:H], rg[:, k:k + 1],
                                                      g_upd[:, :], ALU.mult, ALU.mult)
            L.mark(last)
            for k in range(n):
                last = nc.vector.scalar_tensor_tensor(u_buf[:, k, :], h[:, k, :], omg[:, k:k + 1],
                                                      xr[:, k, :], ALU.mult, ALU.add)
            L.mark(last)
            dve.wait_ge(L.sem, g.times(L.per, 4))
            for k in range(n):
                last = nc.vector.scalar_tensor_tensor(t_buf[:, k, :], be_upd[:, :], gt[:, k:k + 1],
                                                      t_buf[:, k, :], ALU.mult, ALU.add)
            L.mark(last)
            L.wait()
            if before is not None:
                before()
            L.mark(nc.vector.scalar_tensor_tensor(dest, t_buf[:, 0:n, :], 0.0, u_buf[:, 0:n, :],
                                                  ALU.max, ALU.add))

        block = ctx.enter_context(nc.Block())

        @block.sync
        def _(sp):
            sp.wait_ge(s_memset, 1)
            for dest, a in ((src_i, src), (dst_i, dst), (w_f, edge_weight)):
                sp.dma_start(dest[0:FULL, :], a[0:FULL * J].rearrange("(p j) -> p j", j=J)).then_inc(s_e, 16)
                sp.dma_start(dest[FULL:FULL + 1, 0:REST], a[FULL * J:E].rearrange("(p j) -> p j", p=1)).then_inc(s_e, 16)
            sp.dma_start(w_all[:, 0:2, :], msg_w.rearrange("(a p) h -> p a h", p=P)).then_inc(s_w, 16)
            sp.dma_start(w_all[:, 2:4, :], upd_w.rearrange("(a p) h -> p a h", p=P)).then_inc(s_w, 16)
            sp.dma_start(w_u1[:, H:H + 1], gate_w).then_inc(s_w, 16)
            sp.dma_start(bias[0:1, 0, 0:H], msg_b.rearrange("(a h) -> a h", a=1)).then_inc(s_w, 16)
            sp.dma_start(bias[0:1, 0, H:2 * H], upd_b.rearrange("(a h) -> a h", a=1)).then_inc(s_w, 16)
            sp.dma_start(bias[0:1, 0, 2 * H:2 * H + 1], gate_b.rearrange("(a h) -> a h", a=1)).then_inc(s_w, 16)
            for dest, a in ((g_msg, msg_g), (be_msg, msg_beta), (g_upd, upd_g), (be_upd, upd_beta)):
                sp.dma_start(dest[:, :], a.partition_broadcast(P)).then_inc(s_w, 16)
            sp.wait_ge(s_bsplit, 1)
            sp.dma_start(bias3[:, :], bias_b[0:1, :, :]).then_inc(s_b3, 16)

            def base(g):
                return LAST_BASE if g.turn is None and g.at == NG - 1 else g.times(P * G)

            def rows(t, g):
                b = base(g)
                v = t[b:b + P * G, :] if g.turn is None else t[bass.ds(b, P * G), :]
                return v.rearrange("(p k) h -> p k h", k=G)

            def node_step(s, straight):
                if live(s.back(4), NG):
                    g = s.back(4)
                    nd["fin"].after(sp, g)
                    if straight and g.at == NG - 1:
                        q = g.back(1)
                        sp.wait_ge(s_st[q.at % 4], q.rounds(16, 16))
                    sp.dma_start(rows(out, g), o[:, g.at % 4]).then_inc(s_st[g.at % 4], 16)
                if live(s, NG):
                    sp.dma_start(xload[:, s.at % 4], rows(x, s)).then_inc(s_x[s.at % 4], 16)

            run_steps(sp, node_step, NG, 4, 4)

            sums_v = sums_dram.rearrange("(p j) h -> p j h", j=J)

            def edge_step(g, straight):
                ed["sum"].after(sp, g)
                c = g.times(G)
                v = sums_v[:, c:c + G, :] if g.turn is None else sums_v[:, bass.ds(c, G), :]
                sp.dma_start(v, acc[:, g.at % 4]).then_inc(s_sums[g.at % 4], 16)

            run_steps(sp, edge_step, EG, 0, 4)
            for i in range(4):
                sp.wait_ge(s_st[i], 16 * len(range(i, NG, 4)))
                sp.wait_ge(s_sums[i], 16 * len(range(i, EG, 4)))
                sp.wait_ge(s_scat[i], 16 * G * len(range(i, EG, 4)))
            sp.wait_ge(s_to, 16)

        @block.gpsimd
        def _(pool):
            nc.gpsimd.memset(ones[:, :], 1.0)
            nc.gpsimd.memset(eps_col[:, :], EPS)
            nc.gpsimd.memset(ones3[:, :], 1.0)
            nc.gpsimd.iota(tidx[:, 2:3], [[0, 1]], base=0, channel_multiplier=J).then_inc(s_const, 1)
            pool.wait_ge(s_const, 1)
            nc.gpsimd.affine_select(out=ident[:, :], in_=ones[:, :], compare_op=ALU.is_equal, fill=0.0, base=0,
                                    pattern=[[1, P]], channel_multiplier=-1)
            nc.gpsimd.affine_select(out=below[:, :], in_=ones[:, :], compare_op=ALU.is_gt, fill=0.0, base=0,
                                    pattern=[[1, P]], channel_multiplier=-1)
            nc.gpsimd.affine_select(out=above[:, :], in_=ones[:, :], compare_op=ALU.is_gt, fill=0.0, base=0,
                                    pattern=[[-1, P]], channel_multiplier=1).then_inc(s_const, 1)

            pool.wait_ge(s_prep, FLAG)
            unordered = pool.value_load(flag_i[0:1, 0:1], min_val=0, max_val=1)
            with pool.If(unordered > 0):
                pool.dma_start(keys_i[:, 0:E], dst.partition_broadcast(P)).then_inc(s_key, 16)
                pool.wait_ge(s_rank, 1)
                last_row = pool.to_reg(EPAD - 1)
                with pool.Fori(0, J) as t:
                    nc.gpsimd.tensor_copy(stage_r[:, :], rank_i[:, bass.ds(t, 1)])
                    nc.gpsimd.tensor_copy(stage_e[:, :], rec[:, bass.ds(t * 4, 4)]).then_inc(s_stage, 1)
                    pool.wait_ge(s_stage, t + 1)
                    pool.reg_alu(last_row, last_row, EPAD - 1, ALU.min)
                    pool.indirect_dma_start(
                        out=sorted_dram, out_offset=bass.IndirectOffsetOnAxis(ap=stage_r[:, 0:1], axis=0),
                        in_=stage_e[:, :], in_offset=None, bounds_check=last_row, oob_is_err=False,
                    ).then_inc(s_row, 16)
                    pool.wait_ge(s_row, t * 16 + 16)
                pool.dma_start(rec[:, :], sorted_dram.rearrange("(p j) c -> p (j c)", j=J)).then_inc(s_back, 16)
                pool.wait_ge(s_back, 16)
            with pool.Else():
                pool.nop()

            pool.wait_ge(s_prep, INDICES)
            if_tail = dict(bounds_check=N - 1, oob_is_err=False)

            def gather(dest, rows, idx, s):
                pool.indirect_dma_start(out=dest, out_offset=None, in_=rows,
                                        in_offset=bass.IndirectOffsetOnAxis(ap=idx, axis=0),
                                        **(if_tail if rows is x else {})).then_inc(s, 16)

            def scatter(rows, idx, s):
                pool.indirect_dma_start(out=out, out_offset=bass.IndirectOffsetOnAxis(ap=idx, axis=0),
                                        in_=rows, in_offset=None, **if_tail).then_inc(s, 16)

            def gather_group(g):
                if g >= 4:
                    pool.wait_ge(s_gath[g % 4], 2 * G * 16 * (g // 4))
                for part, idx in ((0, src_i), (1, gidx)):
                    for k in range(G):
                        c = g * G + k
                        gather(slot(Group(g), part)[:, k, :], x, idx[:, c:c + 1], s_gath[g % 4])

            for g in range(RING):
                gather_group(g)
            for i in range(4):
                pool.wait_ge(s_st[i], 16 * len(range(i, NG, 4)))
            gather(tail_x, x, tidx[:, 0:1], s_tx)
            for g in range(EG):
                pool.wait_ge(ed["fin"].sem, ed["fin"].per * (g + 1))
                for k in range(G):
                    c = g * G + k
                    scatter(o[:, g % 4, k, :], sidx[:, c:c + 1], s_scat[g % 4])
                if g + RING < EG:
                    gather_group(g + RING)
            for i in range(4):
                pool.wait_ge(s_sums[i], 16 * len(range(i, EG, 4)))
            gather(tail_f, sums_dram, tidx[:, 2:3], s_tf)
            pool.wait_ge(tl["fin"].sem, tl["fin"].per)
            scatter(tail_o, tidx[:, 1:2], s_to)
            pool.wait_ge(s_to, 16)

        @block.vector
        def _(dve):
            prep_n = [0]

            def link(ins):
                prep_n[0] += 1
                ins.then_inc(s_prep, 1)
                dve.wait_ge(s_prep, prep_n[0])

            nc.vector.memset(src_i[:, :], 0)
            nc.vector.memset(dst_i[:, :], NO_NODE)
            nc.vector.memset(w_f[:, :], 0.0).then_inc(s_memset, 1)
            nc.vector.memset(cont[:, :], 0.0)
            link(nc.vector.memset(ones_j, 1.0))
            dve.wait_ge(s_e, 6 * 16)
            dve.wait_ge(s_const, 2)

            def border_columns():
                link(nc.vector.tensor_copy(dst_f, dst_i[:, :]))
                nc.vector.tensor_scalar(dbf, ones[:, :], dst_f[:, 0:1], None, ALU.mult)
                link(nc.vector.tensor_scalar(dbl, ones[:, :], dst_f[:, J - 1:J], None, ALU.mult))

            border_columns()
            assert prep_n[0] == BORDERS1, prep_n
            nc.vector.tensor_tensor(viol[:, 0:J - 1], dst_f[:, 0:J - 1], dst_f[:, 1:J], ALU.is_gt)
            link(nc.vector.memset(viol[:, J - 1:J], 0.0))
            link(nc.vector.reduce_sum(col[:, 0:1], viol, AX.X))
            dve.wait_ge(s_prep_pe, 1)
            link(nc.vector.scalar_tensor_tensor(scr, pm[:, 0, :], dst_f[:, J - 1:J], below[:, :],
                                                ALU.is_lt, ALU.mult, accum_out=col[:, 1:2]))
            link(nc.vector.tensor_tensor(col[:, 2:3], col[:, 0:1], col[:, 1:2], ALU.add))
            assert prep_n[0] == VIOLATIONS, prep_n
            dve.wait_ge(s_prep_pe, 2)
            link(nc.vector.tensor_scalar(flag_i[0:1, 0:1], pm[0:1, 2, 0:1], 1.0, None, ALU.min))
            assert prep_n[0] == FLAG, prep_n
            unordered = dve.value_load(flag_i[0:1, 0:1], min_val=0, max_val=1)
            with dve.If(unordered > 0):
                fall = [0]

                def flink(ins, n=None):
                    fall[0] += 1
                    ins.then_inc(s_fall, 1)
                    dve.wait_ge(s_fall, fall[0] if n is None else n)

                nc.vector.memset(keys[:, E:EPAD], float(NO_NODE))
                nc.vector.memset(rec[:, :], 0)
                dve.wait_ge(s_key, 16)
                flink(nc.vector.tensor_copy(keys[:, 0:E], keys_i[:, 0:E]))
                key_cols = keys[:, :].rearrange("p (q j) -> p q j", j=J)
                half = EPAD // 2
                with dve.Fori(0, J) as t:
                    d = dst_f[:, bass.ds(t, 1)]
                    for m in range(2):
                        nc.vector.tensor_scalar(smaller[:, :], keys[:, m * half:(m + 1) * half], d, None,
                                                ALU.is_lt, ALU.add, accum_out=col[:, 4 + m:5 + m])
                    nc.vector.scalar_tensor_tensor(scr, key_cols[:, :, bass.ds(t, 1)].rearrange("p q a -> p (q a)"), d,
                                                   above[:, :], ALU.is_equal, ALU.mult,
                                                   accum_out=col[:, 6:7]).then_inc(s_fall, 1)
                    dve.wait_ge(s_fall, t * 3 + 2)
                    nc.vector.tensor_scalar(key_cols[:, :, bass.ds(t, 1)], key_cols[:, :, bass.ds(t, 1)], 0.5, None,
                                            ALU.subtract)
                    nc.vector.tensor_tensor(col[:, 7:8], col[:, 4:5], col[:, 5:6], ALU.add).then_inc(s_fall, 1)
                    dve.wait_ge(s_fall, t * 3 + 3)
                    nc.vector.tensor_tensor(rank_i[:, bass.ds(t, 1)], col[:, 7:8], col[:, 6:7],
                                            ALU.add).then_inc(s_fall, 1)
                    dve.wait_ge(s_fall, t * 3 + 4)
                rec_v = rec[:, :].rearrange("p (j c) -> p j c", c=4)
                nc.vector.tensor_copy(rec_v[:, :, 0], src_i[:, :])
                nc.vector.tensor_copy(rec_v[:, :, 1], dst_i[:, :])
                nc.vector.tensor_copy(rec_v[:, :, 2].bitcast(f32), w_f[:, :]).then_inc(s_rank, 1)
                dve.wait_ge(s_back, 16)
                nc.vector.tensor_copy(src_i[:, :], rec_v[:, :, 0])
                nc.vector.tensor_copy(dst_i[:, :], rec_v[:, :, 1])
                nc.vector.tensor_copy(w_f[:, :], rec_v[:, :, 2].bitcast(f32)).then_inc(s_rank, 1)
                dve.wait_ge(s_rank, 2)
            with dve.Else():
                nc.vector.memset(col[:, 8:9], 0.0)

            border_columns()
            assert prep_n[0] == BORDERS2, prep_n
            link(nc.vector.tensor_tensor(cont[:, 1:J], dst_f[:, 1:J], dst_f[:, 0:J - 1], ALU.is_equal))
            nc.vector.tensor_tensor_scan(run_f, cont[:, 0:J], ones_j, 0.0, ALU.mult, ALU.add)
            nc.vector.tensor_tensor_scan(run_b[:, ::-1], cont[:, 1:J + 1][:, ::-1], ones_j, 0.0, ALU.mult, ALU.add)
            nc.vector.tensor_scalar(is_first, dst_f, dst_f[:, 0:1], None, ALU.is_equal)
            link(nc.vector.tensor_scalar(is_last, dst_f, dst_f[:, J - 1:J], None, ALU.is_equal))
            nc.vector.tensor_copy(col[:, 9:10], run_f[:, J - 1:J])
            link(nc.vector.reduce_sum(col[:, 10:11], is_first, AX.X))
            dve.wait_ge(s_prep_pe, 3)
            nc.vector.scalar_tensor_tensor(carry_m[:, :], pm[:, 0, :], dst_f[:, J - 1:J], below[:, :],
                                           ALU.is_equal, ALU.mult)
            link(nc.vector.scalar_tensor_tensor(m2, pm[:, 1, :], dst_f[:, 0:1], above[:, :],
                                                ALU.is_equal, ALU.mult))
            assert prep_n[0] == MATRICES, prep_n
            link(nc.vector.tensor_tensor(cnt, run_f, run_b, ALU.add))
            dve.wait_ge(s_prep_pe, 4)
            link(nc.vector.tensor_copy(col[:, 12:14], pm[:, 2, 0:2]))
            before_n, after_n = col[:, 12:13], col[:, 13:14]
            link(nc.vector.scalar_tensor_tensor(cnt, is_first, before_n, cnt, ALU.mult, ALU.add))
            link(nc.vector.scalar_tensor_tensor(cnt, is_last, after_n, cnt, ALU.mult, ALU.add))
            link(nc.vector.tensor_scalar(cnt, cnt, -1.0, None, ALU.add))
            nc.vector.tensor_scalar(col[:, 14:15], before_n, 0.0, None, ALU.is_gt)
            nc.vector.tensor_scalar(col[:, 15:16], after_n, 0.0, None, ALU.is_gt)
            link(nc.vector.reciprocal(wb[:, :], cnt))
            nc.vector.tensor_scalar(col[:, 16:17], col[:, 10:11], float(J), None, ALU.is_equal)
            nc.vector.tensor_tensor(wb[:, :], wb[:, :], w_f[:, :], ALU.mult)
            nc.vector.tensor_scalar(ok[:, 0:J - 1], cont[:, 1:J], -1.0, 1.0, ALU.mult, ALU.add)
            nc.vector.tensor_scalar(ok[:, J - 1:J], col[:, 15:16], -1.0, 1.0, ALU.mult, ALU.add)
            link(nc.vector.tensor_scalar(is_first, is_first, col[:, 14:15], None, ALU.mult))
            nc.vector.tensor_tensor(col[:, 17:18], col[:, 16:17], col[:, 15:16], ALU.mult)
            link(nc.vector.tensor_scalar(is_first, is_first, -1.0, 1.0, ALU.mult, ALU.add))
            nc.vector.tensor_scalar(col[:, 18:19], col[:, 17:18], -1.0, 1.0, ALU.mult, ALU.add)
            link(nc.vector.tensor_tensor(ok, ok, is_first, ALU.mult))
            nc.vector.tensor_tensor(col[:, 19:20], col[:, 18:19], col[:, 14:15], ALU.mult)
            link(nc.vector.scalar_tensor_tensor(ok, dst_f, float(N), ok, ALU.is_lt, ALU.mult))
            nc.vector.tensor_scalar(col[:, 20:21], col[:, 19:20], -FAR, FAR, ALU.mult, ALU.add)
            link(nc.vector.tensor_scalar(ok, ok, -FAR, FAR, ALU.mult, ALU.add))
            nc.vector.tensor_tensor(sidx[:, :], dst_f, ok, ALU.add)
            nc.vector.tensor_tensor(tidx[:, 1:2], dst_f[:, 0:1], col[:, 20:21], ALU.add)
            nc.vector.tensor_copy(tidx[:, 0:1], dst_f[:, 0:1])
            nc.vector.scalar_tensor_tensor(tidx[:, 2:3], col[:, 10:11], -1.0, tidx[:, 2:3], ALU.add, ALU.add)
            link(nc.vector.tensor_scalar(gidx[:, :], dst_f, float(N - 1), None, ALU.min))
            assert prep_n[0] == INDICES, prep_n

            dve.wait_ge(s_w, 10 * 16)
            nc.vector.reduce_sum(bias_sum[0:1, 0:2], bias[0:1, 0, 0:2 * H].rearrange("p (a h) -> p a h", a=2), AX.X)
            link(nc.vector.reduce_sum(wmean[:, :], w_all[:, :, :], AX.X))
            nc.vector.tensor_scalar(bias_sum[0:1, :], bias_sum[0:1, :], 1.0 / H, None, ALU.mult)
            link(nc.vector.tensor_scalar(wmean[:, :], wmean[:, :], 1.0 / H, None, ALU.mult))
            for a in range(4):
                nc.vector.tensor_scalar(w_all[:, a, :], w_all[:, a, :], wmean[:, a:a + 1], None, ALU.subtract)
            for a in range(2):
                last = nc.vector.tensor_scalar(bias[0:1, 0, a * H:(a + 1) * H], bias[0:1, 0, a * H:(a + 1) * H],
                                               bias_sum[0:1, a:a + 1], None, ALU.subtract)
            link(last)
            nc.vector.tensor_copy(w_u1[:, 0:H], w_all[:, 2, :])
            link(nc.vector.tensor_copy(bias_b[0:1, 0, :], bias[0:1, 0, :]))
            link(nc.vector.tensor_tensor(bias[0:1, 1, :], bias[0:1, 0, :], bias_b[0:1, 0, :], ALU.subtract))
            link(nc.vector.tensor_copy(bias_b[0:1, 1, :], bias[0:1, 1, :]))
            link(nc.vector.tensor_tensor(bias[0:1, 2, :], bias[0:1, 1, :], bias_b[0:1, 1, :], ALU.subtract))
            nc.vector.tensor_copy(bias_b[0:1, 2, :], bias[0:1, 2, :]).then_inc(s_bsplit, 1)
            dve.wait_ge(s_bsplit, 1)
            assert prep_n[0] == WEIGHTS, prep_n

            def node_xn(g):
                return rows4(xn[:, (g.at % 4) * G * H:(g.at % 4 + 1) * G * H])

            def node_step(s, straight):
                if live(s, NG):
                    dve.wait_ge(s_x[s.at % 4], s.rounds(16, 16))
                    do_stats(dve, nd["stats"], s, [xload[:, s.at % 4]])
                g = s.back(1)
                if live(g, NG):
                    nd["rstd"].after(dve, g)
                    L = nd["norm"]
                    L.begin(dve, g)
                    L.mark(normalise(g, node_xn(g), xload[:, g.at % 4], 0))
                    L.wait()
                    L.mark(nc.vector.tensor_scalar(node_xn(g), node_xn(g), 0.0, None, ALU.max))
                g = s.back(3)
                if live(g, NG):
                    def stored():
                        if g.turn is not None or g.at >= 4:
                            dve.wait_ge(s_st[g.at % 4], g.rounds(16))
                    do_fin(dve, nd, g, node_xn(g), xload[:, g.at % 4], o[:, g.at % 4], G, stored)

            run_steps(dve, node_step, NG, 3, 8)

            nc.vector.memset(acc[:, 3, G - 1, :], 0.0).then_inc(s_bsplit, 1)
            dve.wait_ge(s_bsplit, 2)

            def edge_xn(g):
                return rows4(xn[:, (g.at % 2) * 2 * G * H:(g.at % 2 + 1) * 2 * G * H])

            def edge_sums(g):
                ed["mstd"].after(dve, g)
                if g.turn is not None or g.at >= 2:
                    ed["fin"].after(dve, g.back(2))
                L = ed["sum"]
                L.begin(dve, g)
                for k in range(G):
                    last = nc.vector.scalar_tensor_tensor(t_buf[:, k, :], pm[:, k, :], rm[:, g.at % 2, k:k + 1],
                                                          g_msg[:, :], ALU.mult, ALU.mult)
                L.mark(last)
                L.wait()
                L.mark(nc.vector.tensor_tensor(t_buf[:, :, :], t_buf[:, :, :],
                                               be_msg[:, :].unsqueeze(1).to_broadcast([P, G, H]), ALU.add))
                L.wait()
                c = g.times(G) if g.turn is None else dve.snap(g.times(G))
                for k in range(G):
                    last = nc.vector.tensor_scalar(t_buf[:, k, :], t_buf[:, k, :], 0.0, column(wb, c, k),
                                                   ALU.max, ALU.mult)
                L.mark(last)
                if g.turn is not None or g.at >= 4:
                    dve.wait_ge(s_sums[g.at % 4], g.rounds(16))
                L.wait()
                before = acc[:, (g.at - 1) % 4, G - 1, :]
                for k in range(G):
                    L.mark(nc.vector.scalar_tensor_tensor(acc[:, g.at % 4, k, :], before, column(cont, c, k),
                                                          t_buf[:, k, :], ALU.mult, ALU.add))
                    L.wait()
                    before = acc[:, g.at % 4, k, :]

            def edge_step(s, straight):
                if live(s, EG):
                    dve.wait_ge(s_gath[s.at % 4], s.rounds(2 * G * 16, 2 * G * 16))
                    at = slot_base(dve, s)
                    do_stats(dve, ed["stats"], s, [slot(s, 0, at), slot(s, 1, at)])
                g = s.back(1)
                if live(g, EG):
                    ed["rstd"].after(dve, g)
                    L = ed["norm"]
                    L.begin(dve, g)
                    v = edge_xn(g)
                    at = slot_base(dve, g)
                    normalise(g, v, slot(g, 0, at), 0)
                    L.mark(normalise(g, v, slot(g, 1, at), G))
                    L.wait()
                    L.mark(nc.vector.tensor_scalar(slot(g, 0, at), v[:, G:2 * G, :], 0.0, None, ALU.max))
                g = s.back(4)
                if live(g, EG):
                    def scattered():
                        if g.turn is not None or g.at >= 4:
                            dve.wait_ge(s_scat[g.at % 4], g.rounds(16 * G))
                        elif g.at < 4:
                            dve.wait_ge(s_st[g.at % 4], 16 * len(range(g.at % 4, NG, 4)))
                    at = slot_base(dve, g)
                    do_fin(dve, ed, g, slot(g, 0, at), slot(g, 1, at), o[:, g.at % 4], G, scattered)
                g = s.back(2)
                if live(g, EG):
                    edge_sums(g)

            run_steps(dve, edge_step, EG, 4, 9)

            z = Group(0)
            dve.wait_ge(s_tx, 16)
            tx, th = tail_x.unsqueeze(1), tail_h.unsqueeze(1)
            do_stats(dve, tl["stats"], z, [tx])
            tl["rstd"].after(dve, z)
            L = tl["norm"]
            L.begin(dve, z)
            L.mark(normalise(z, th, tx, 0))
            L.wait()
            L.mark(nc.vector.tensor_scalar(th, th, 0.0, None, ALU.max))
            tl["msg"].after(dve, z)
            dve.wait_ge(s_tf, 16)
            L = tl["sum"]
            L.begin(dve, z)
            L.mark(nc.vector.tensor_tensor(tail_a, pm[:, 0, :], tail_f, ALU.add))
            do_fin(dve, tl, z, th, tx, tail_o.unsqueeze(1), 1)

        @block.scalar
        def _(act):
            nc.scalar.preload_act_table_set("natural_log_exp_and_others")

            def evacuate(d, g, dest, source, func, stage, flip):
                d[flip].after(act, g)
                L = d[stage]
                L.begin(act, g)
                L.mark(nc.scalar.activation(dest, source, func))

            def node_step(s, straight):
                if live(s, NG):
                    do_rstd(act, nd, s, G)
                g = s.back(2)
                if live(g, NG):
                    do_post(act, nd, g, G)
                g = s.back(1)
                if live(g, NG):
                    evacuate(nd, g, ht[:, g.at % 4, 0:G * H], pt[:, g.at % 2, :], ACT.Copy, "ht", "flip")

            run_steps(act, node_step, NG, 2, 4)

            def edge_step(s, straight):
                if live(s, EG):
                    do_rstd(act, ed, s, 2 * G)
                g = s.back(2)
                if live(g, EG):
                    ed["msg"].after(act, g)
                    L = ed["mstd"]
                    L.begin(act, g)
                    b = g.at % 2
                    for k in range(G):
                        last = nc.scalar.activation(junkm[:, b, k, :], pm[:, k, :], ACT.Square, accum_out=ssm[:, b, k:k + 1])
                    L.mark(last)
                    L.wait()
                    L.mark(nc.scalar.activation(lnm[:, b, :], ssm[:, b, :], ACT.Ln, bias=eps_col[:, :], scale=1.0 / H))
                    L.wait()
                    L.mark(nc.scalar.activation(rm[:, b, :], lnm[:, b, :], ACT.Exp, scale=-0.5))
                g = s.back(3)
                if live(g, EG):
                    do_post(act, ed, g, G)
                g = s.back(1)
                if live(g, EG):
                    evacuate(ed, g, ht[:, g.at % 4, :], pt[:, :, :].rearrange("p a b -> p (a b)"), ACT.Relu, "ht", "flip")
                g = s.back(2)
                if live(g, EG):
                    evacuate(ed, g, at_[:, g.at % 2, :], pa[:, :], ACT.Copy, "at", "aflip")

            run_steps(act, edge_step, EG, 3, 5)

            z = Group(0)
            do_rstd(act, tl, z, 1)
            evacuate(tl, z, ht[:, 2, 0:H], pt[:, 0, 0:H], ACT.Copy, "ht", "flip")
            evacuate(tl, z, at_[:, 1, 0:H], pa[:, 0:H], ACT.Copy, "at", "aflip")
            do_post(act, tl, z, 1)

        @block.tensor
        def _(pe):
            def flip(dest, rows):
                for k in range(rows.shape[1]):
                    last = nc.tensor.transpose(dest[:, k * H:(k + 1) * H], rows[:, k, :], ident[:, :])
                return last

            def add_bias(dest, lo, hi):
                return nc.tensor.matmul(dest, ones3[:, :], bias3[:, lo:hi], start=False, stop=True)

            def spread(dest, column_spread):
                return nc.tensor.matmul(dest, column_spread, ident[:, :], start=True, stop=True)

            pe.wait_ge(s_const, 2)
            pe.wait_ge(s_prep, BORDERS1)
            spread(pm[:, 0, :], dbf).then_inc(s_prep_pe, 1)
            pe.wait_ge(s_prep, VIOLATIONS)
            nc.tensor.matmul(pm[0:1, 2, 0:1], col[:, 2:3], ones[:, 0:1], start=True, stop=True).then_inc(s_prep_pe, 1)
            pe.wait_ge(s_prep, BORDERS2)
            spread(pm[:, 0, :], dbf)
            spread(pm[:, 1, :], dbl).then_inc(s_prep_pe, 1)
            pe.wait_ge(s_prep, MATRICES)
            nc.tensor.matmul(pm[:, 2, 0:1], carry_m[:, :], col[:, 9:10], start=True, stop=True)
            nc.tensor.matmul(pm[:, 2, 1:2], m2, col[:, 10:11], start=True, stop=True).then_inc(s_prep_pe, 1)
            pe.wait_ge(s_b3, 16)
            pe.wait_ge(s_prep, WEIGHTS)

            def node_step(s, straight):
                g = s.back(2)
                if live(g, NG):
                    nd["ht"].after(pe, g)
                    if g.turn is not None or g.at >= 2:
                        nd["fin"].after(pe, g.back(2))
                    for k in range(G):
                        nc.tensor.matmul(py[:, g.at % 2, k, 0:H + 1], ht[:, g.at % 4, k * H:(k + 1) * H], w_u1[:, :],
                                         start=True, stop=False)
                        last = add_bias(py[:, g.at % 2, k, 0:H + 1], H, 2 * H + 1)
                    nd["upd"].begin(pe, g)
                    nd["upd"].mark(last)
                g = s.back(1)
                if live(g, NG):
                    nd["norm"].after(pe, g)
                    if g.turn is not None or g.at >= 2:
                        nd["ht"].after(pe, g.back(2))
                    nd["flip"].begin(pe, g)
                    nd["flip"].mark(flip(pt[:, g.at % 2, :], rows4(xn[:, (g.at % 4) * G * H:(g.at % 4 + 1) * G * H])))

            run_steps(pe, node_step, NG, 2, 4)

            def edge_step(s, straight):
                g = s.back(2)
                if live(g, EG):
                    ed["ht"].after(pe, g)
                    if g.turn is not None or g.at >= 1:
                        ed["sum"].after(pe, g.back(1), 1)
                    for k in range(G):
                        nc.tensor.matmul(pm[:, k, :], ht[:, g.at % 4, k * H:(k + 1) * H], w_all[:, 0, :],
                                         start=True, stop=False)
                        nc.tensor.matmul(pm[:, k, :], ht[:, g.at % 4, (G + k) * H:(G + k + 1) * H], w_all[:, 1, :],
                                         start=False, stop=False)
                        last = add_bias(pm[:, k, :], 0, H)
                    ed["msg"].begin(pe, g)
                    ed["msg"].mark(last)
                g = s.back(3)
                if live(g, EG):
                    ed["at"].after(pe, g)
                    if g.turn is not None or g.at >= 2:
                        ed["fin"].after(pe, g.back(2))
                    else:
                        nd["fin"].after(pe, Group(NG - 1))
                    for k in range(G):
                        nc.tensor.matmul(py[:, g.at % 2, k, 0:H + 1], ht[:, g.at % 4, (G + k) * H:(G + k + 1) * H],
                                         w_u1[:, :], start=True, stop=False)
                        nc.tensor.matmul(py[:, g.at % 2, k, 0:H], at_[:, g.at % 2, k * H:(k + 1) * H], w_all[:, 3, :],
                                         start=False, stop=False)
                        last = add_bias(py[:, g.at % 2, k, 0:H + 1], H, 2 * H + 1)
                    ed["upd"].begin(pe, g)
                    ed["upd"].mark(last)
                g = s.back(1)
                if live(g, EG):
                    ed["norm"].after(pe, g, 1)
                    if g.turn is not None or g.at >= 1:
                        ed["ht"].after(pe, g.back(1))
                    ed["flip"].begin(pe, g)
                    ed["flip"].mark(flip(pt[:, :, :].rearrange("p a b -> p (a b)"),
                                         rows4(xn[:, (g.at % 2) * 2 * G * H:(g.at % 2 + 1) * 2 * G * H])))
                g = s.back(2)
                if live(g, EG):
                    ed["sum"].after(pe, g)
                    if g.turn is not None or g.at >= 1:
                        ed["at"].after(pe, g.back(1))
                    ed["aflip"].begin(pe, g)
                    ed["aflip"].mark(flip(pa[:, :], acc[:, g.at % 4]))

            run_steps(pe, edge_step, EG, 3, 5)

            z = Group(0)
            nc.tensor.matmul(pm[:, 0, :], carry_m[:, :], acc[:, (EG - 1) % 4, G - 1, :], start=True, stop=True
                             ).then_inc(tl["msg"].sem, 1)
            tl["norm"].after(pe, z)
            nc.tensor.transpose(pt[:, 0, 0:H], tail_h, ident[:, :]).then_inc(tl["flip"].sem, 1)
            pe.wait_ge(tl["sum"].sem, 1)
            nc.tensor.transpose(pa[:, 0:H], tail_a, ident[:, :]).then_inc(tl["aflip"].sem, 1)
            tl["ht"].after(pe, z)
            tl["at"].after(pe, z)
            ed["fin"].after(pe, Group(EG - 1))
            nc.tensor.matmul(py[:, 0, 0, 0:H + 1], ht[:, 2, 0:H], w_u1[:, :], start=True, stop=False)
            nc.tensor.matmul(py[:, 0, 0, 0:H], at_[:, 1, 0:H], w_all[:, 3, :], start=False, stop=False)
            add_bias(py[:, 0, 0, 0:H + 1], H, 2 * H + 1).then_inc(tl["upd"].sem, 1)


INPUTS = ["x", "src", "dst", "edge_weight"] + ["L0_gnn_" + n for n in (
    "msg_w", "msg_b", "msg_g", "msg_beta", "upd_w", "upd_b", "upd_g", "upd_beta", "gate_w", "gate_b")]


def kernel(**inputs):
    import numpy as np
    import concourse.bacc as bacc
    from concourse.bass_utils import run_bass_kernel_spmd

    nc = bacc.Bacc("TRN2", target_bir_lowering=False, num_devices=1)
    arrays, args = {}, []
    for name in INPUTS:
        a = np.ascontiguousarray(inputs[name])
        arrays[f"in_{name}"] = a
        args.append(nc.dram_tensor(f"in_{name}", a.shape, mybir.dt.from_np(a.dtype), kind="ExternalInput").ap())
    out = nc.dram_tensor("out", (N, H), f32, kind="ExternalOutput").ap()
    build(nc, *args, out)
    r = run_bass_kernel_spmd(nc, [arrays], core_ids=[0])
    return r.results[0]["out"]
```

```python
from contextlib import ExitStack

import concourse.bass as bass
from concourse import mybir

N, E, H = 50000, 25000, 128
P = 128
G = 4
NG = -(-N // (P * G))
LAST_BASE = N - P * G
J = 196
EG = J // G
EPAD = P * J
FULL = E // J
REST = E - FULL * J
RING = 30
EPS = 1e-5
FAR = float(1 << 20)
NO_NODE = 1 << 17
XS = 8

BORDERS1, VIOLATIONS, FLAG, BORDERS2, MATRICES, INDICES, WEIGHTS = 3, 7, 8, 10, 14, 26, 33

f32, bf16, i32 = mybir.dt.float32, mybir.dt.bfloat16, mybir.dt.int32
u32, u8 = mybir.dt.uint32, mybir.dt.uint8
ALU, ACT, AX = mybir.AluOpType, mybir.ActivationFunctionType, mybir.AxisListType


class Group:

    def __init__(self, at, turn=None, un=0):
        self.at, self.turn, self.un = at, turn, un

    def back(self, k):
        return Group(self.at - k, self.turn, self.un)

    def times(self, c, d=0):
        return c * self.at + d if self.turn is None else self.turn * (c * self.un) + (c * self.at + d)

    def rounds(self, c, d=0, ring=4):
        a = c * (self.at // ring) + d
        return a if self.turn is None else self.turn * (c * self.un // ring) + a


class Steps:

    def __init__(self, sem, per):
        self.sem, self.per, self.eng, self.g, self.n = sem, per, None, None, 0

    def begin(self, eng, g):
        self.eng, self.g, self.n = eng, g, 0

    def mark(self, ins):
        self.n += 1
        assert self.n <= self.per
        ins.then_inc(self.sem, 1)

    def wait(self):
        self.eng.wait_ge(self.sem, self.g.times(self.per, self.n))

    def after(self, eng, g, n=None):
        eng.wait_ge(self.sem, g.times(self.per, self.per if n is None else n))


def run_steps(eng, step, n_groups, skew, lead, un):
    turns = (n_groups - 1 - lead) // un
    stop = lead + turns * un
    for s in range(lead):
        step(Group(s))
    with eng.Fori(0, turns) as i:
        for u in range(un):
            step(Group(lead + u, i, un))
    for s in range(stop, n_groups + skew):
        step(Group(s))


def live(g, n_groups):
    return g.turn is not None or 0 <= g.at < n_groups


def beyond(g, n):
    return g.turn is not None or g.at >= n


def build(nc, x, src, dst, edge_weight, msg_w, msg_b, msg_g, msg_beta, upd_w, upd_b, upd_g, upd_beta,
          gate_w, gate_b, out):
    ctx = ExitStack()
    nc.disable_value_cache = True
    with ctx:
        def sb(name, shape, dt=f32):
            return ctx.enter_context(nc.sbuf_tensor(name, shape, dt))

        def sem(name):
            return ctx.enter_context(nc.semaphore(name))

        def sem4(name):
            return [sem(f"{name}{i}") for i in range(4)]

        sums_dram = nc.dram_tensor("running_sums", (EPAD, H), f32).ap()
        sorted_dram = nc.dram_tensor("sorted_edges", (EPAD, 4), i32).ap()

        ring = sb("ring", [P, RING * 2 * G * H])
        work = sb("work", [P, 14 * G * H])
        o = work[:, 0:4 * G * H].rearrange("p (a k h) -> p a k h", a=4, h=H)
        t_buf = work[:, 4 * G * H:8 * G * H].rearrange("p (a k h) -> p a k h", a=4, h=H)
        ht_dst = work[:, 8 * G * H:12 * G * H].rearrange("p (a f) -> p a f", a=4)
        ht_src = work[:, 12 * G * H:14 * G * H].rearrange("p (a f) -> p a f", a=2)
        hrow = sb("hrow", [P, 4, G, H])
        acc = sb("acc", [P, 4, G, H])
        at_ = sb("at", [P, 2, G * H])
        xload = sb("xload", [P, XS, G, H])
        junk = sb("junk", [P, 2, G, H], bf16)
        w_all = sb("w_all", [P, 4, H])
        w_u1 = sb("w_u1", [P, H + 1])
        g_msg = sb("g_msg", [P, H])
        be_msg = sb("be_msg", [P, H])
        g_upd = sb("g_upd", [P, H])
        be_upd = sb("be_upd", [P, H])
        ident = sb("ident", [P, P])
        ones = hrow[:, 0, 0, :]
        below = hrow[:, 0, 1, :]
        above = hrow[:, 0, 2, :]
        bias = hrow[0:1, 1:4, :, :].rearrange("p a b h -> p (a b h)")[:, 0:3 * (2 * H + 1)].rearrange(
            "p (c h) -> p c h", c=3)
        bias_sum = sb("bias_sum", [1, 2])
        bias_b = sb("bias_b", [1, 3, 2 * H + 1], bf16)
        bias3 = sb("bias3", [3, 2 * H + 1], bf16)
        ones3 = sb("ones3", [3, P], bf16)
        wmean = sb("wmean", [P, 4])
        st = sb("st", [P, 4, 2 * G, 6])
        mv = sb("mv", [P, 4, 16, 2])
        lnv = sb("lnv", [P, 4, 16])
        rs = sb("rs", [P, 4, 16])
        nb = sb("nb", [P, 4, 2 * G])
        ge = sb("ge", [P, 2, G])
        e1 = sb("e1", [P, 4, G])
        gt = sb("gt", [P, 4, G])
        omg = sb("omg", [P, 4, G])
        src_i = sb("src_i", [P, J], i32)
        dst_i = sb("dst_i", [P, J], i32)
        w_f = sb("w_f", [P, J])
        gidx = sb("gidx", [P, J], i32)
        sidx = sb("sidx", [P, J], i32)
        cont = sb("cont", [P, J + 1])
        wb = sb("wb", [P, J])
        carry_m = sb("carry_m", [P, P])
        tidx = sb("tidx", [P, 3], i32)
        flag_i = sb("flag_i", [1, 1], i32)
        eps_col = sb("eps_col", [P, 1])
        prep = acc[:, :, :, :].rearrange("p a b c -> p (a b c)")

        def pre(i, n=J):
            return prep[:, i * (J + 4):i * (J + 4) + n]

        dst_f, ones_j, run_f, run_b, is_first, is_last, cnt, ok, viol = (pre(i) for i in range(9))
        m2 = at_[:, 0, 0:P]
        dbf = at_[:, 0, P:2 * P]
        dbl = at_[:, 0, 2 * P:3 * P]
        scr = at_[:, 1, 0:P]
        col = at_[:, 1, P:P + 32]

        h_dst = xload

        TAIL_SLOT = EG - RING
        tail_x, tail_h, tail_f, tail_a, tail_o = (
            ring[:, (TAIL_SLOT * 2 * G + k) * H:(TAIL_SLOT * 2 * G + k + 1) * H] for k in range(5))

        keys = ring[:, 0:EPAD]
        keys_i = keys.bitcast(i32)
        smaller = work[:, 0:EPAD // 4].bitcast(u8)
        spare = ring[:, EPAD:EPAD + 5 * J + 8].bitcast(i32)
        rank_i = spare[:, 0:J]
        rec = spare[:, J:5 * J]
        stage_r, stage_e = spare[:, 5 * J:5 * J + 1], spare[:, 5 * J + 4:5 * J + 8]

        pt = ctx.enter_context(nc.psum_tensor("pt", [P, 2, G * H], f32))
        pm = ctx.enter_context(nc.psum_tensor("pm", [P, G, H], f32))
        pa = ctx.enter_context(nc.psum_tensor("pa", [P, G * H], f32))
        py = ctx.enter_context(nc.psum_tensor("py", [P, 2, G, 2 * H], f32))

        s_w = sem("weights_loaded")
        s_e = sem("edges_loaded")
        s_memset = sem("edge_pads_set")
        s_const = sem("constants_built")
        s_prep = sem("prep_done_by_vector")
        s_prep_pe = sem("prep_done_by_tensor")
        s_wready = sem("weights_centred")
        s_b3 = sem("bias_parts_placed")
        s_bsplit = sem("bias_parts_split")
        s_key = sem("sort_keys_loaded")
        s_rank = sem("edges_ranked")
        s_stage = sem("sort_row_staged")
        s_row = sem("sort_row_written")
        s_back = sem("sorted_edges_loaded")
        s_fall = sem("vector_steps_of_sort")
        s_x = [sem(f"x_loaded{i}") for i in range(XS)]
        s_st = sem4("node_rows_stored")
        s_gath = sem4("rows_gathered")
        s_scat = sem4("rows_scattered")
        s_sums = sem4("running_sums_stored")
        s_tx, s_tf, s_to = sem("tail_x_gathered"), sem("tail_sums_gathered"), sem("tail_scattered")

        def stages(kind, names):
            return {n: Steps(sem(f"{kind}_{n}"), per) for n, per in names.items()}

        common = {
            "stats": 2,
            "nb": 1,
            "gain": 3,
            "mix": 1,
            "gamma": 1, "beta": 1,
            "ln": 1, "rstd": 1,
            "h": 1,
            "ht": 1,
            "post": 1,
            "relu": 1,
            "final": 1,
            "flip": 1,
            "upd": 1,
        }
        nd = stages("node", common)
        tl = stages("tail", common)
        tl.update(stages("tail", {"msg": 1, "sum": 1, "aflip": 1, "at": 1}))
        ed = stages("edge", {**common, "h": 2, "ht": 1,
                             "gamma_m": 1, "beta_m": 1,
                             "msgw": 1,
                             "sum": G,
                             "square_m": 1,
                             "at": 1,
                             "msg": 1,
                             "aflip": 1})

        def rows4(v):
            return v.rearrange("p (k h) -> p k h", h=H)

        def slot(g, part, base=None, n=G):
            if g.turn is None:
                a = (g.at % RING) * 2 * G * H + part * G * H
                return rows4(ring[:, a:a + n * H])
            return rows4(ring[:, bass.ds(base + part * G * H, n * H)])

        def slot_base(eng, g):
            return None if g.turn is None else eng.snap((g.times(1) % RING) * (2 * G * H))

        def column(t, c, k):
            return t[:, c + k:c + k + 1] if isinstance(c, int) else t[:, bass.ds(c + k, 1)]

        def one_mark(L, eng, g, ins):
            L.begin(eng, g)
            L.mark(ins)

        def row_stats(L, g, rows, at):
            for m in range(rows.shape[1]):
                last = nc.vector.bn_stats(st[:, g.at % 4, at + m, :], rows[:, m, :])
            return last

        def aggregate(L, g, n):
            for m in range(n):
                last = nc.vector.bn_aggr(mv[:, (g.at + 1) % 4, m, :], st[:, g.at % 4, m, :])
            L.mark(last)

        def logs(act, d, s, k):
            one_mark(d["ln"], act, s, nc.scalar.activation(lnv[:, s.at % 4, 0:k], mv[:, s.at % 4, 0:k, 1], ACT.Ln,
                                                           bias=eps_col[:, :]))

        def rstds(act, d, s, k):
            act.wait_ge(d["ln"].sem, s.times(1, 1))
            one_mark(d["rstd"], act, s, nc.scalar.activation(rs[:, s.at % 4, 0:k], lnv[:, s.at % 4, 0:k], ACT.Exp,
                                                             scale=-0.5))

        def minus_mean(dve, d, g, n):
            d["rstd"].after(dve, g.back(-1))
            s4 = (g.at + 1) % 4
            one_mark(d["nb"], dve, g, nc.vector.scalar_tensor_tensor(
                nb[:, s4, 0:n], mv[:, s4, 0:n, 0], -1.0, rs[:, s4, 0:n], ALU.mult, ALU.mult))

        def h_rows(g, dest, rows, at):
            s4 = (g.at + 1) % 4
            for m in range(rows.shape[1]):
                last = nc.scalar.activation(dest[:, m, :], rows[:, m, :], ACT.Relu, bias=nb[:, s4, at + m:at + m + 1],
                                            scale=rs[:, s4, at + m:at + m + 1])
            return last

        def squares(prod, slot, at, n=G, j=0):
            for k in range(n):
                last = nc.scalar.activation(junk[:, j, k, :], prod[:, k, 0:H], ACT.Square, scale=float(H) ** -0.5,
                                            accum_out=mv[:, slot, at + k, 1:2])
            return last

        def post(act, d, g, slot, at, n=G):
            d["upd"].after(act, g)
            squares(py[:, g.at % 2], slot, at, n)
            one_mark(d["post"], act, g, nc.scalar.activation(ge[:, g.at % 2, 0:n], py[:, g.at % 2, 0:n, H], ACT.Exp,
                                                             scale=-1.0))

        def gated_relu(act, d, g, n=G):
            d["beta"].after(act, g)
            for k in range(n):
                last = nc.scalar.activation(t_buf[:, g.at % 4, k, :], t_buf[:, g.at % 4, k, :], ACT.Relu,
                                            scale=gt[:, g.at % 4, k:k + 1])
            one_mark(d["relu"], act, g, last)

        def gain(dve, d, g, which, n=G):
            L, b = d["gain"], g.at % 4
            if which == 0:
                d["post"].after(dve, g)
                L.begin(dve, g)
                L.mark(nc.vector.tensor_scalar(e1[:, b, 0:n], ge[:, g.at % 2, 0:n], 1.0, None, ALU.add))
            elif which == 1:
                L.wait()
                L.mark(nc.vector.reciprocal(gt[:, b, 0:n], e1[:, b, 0:n]))
            else:
                L.wait()
                L.mark(nc.vector.tensor_scalar(omg[:, b, 0:n], gt[:, b, 0:n], -1.0, 1.0, ALU.mult, ALU.add))

        def mix_row(g, k, h, xr, dest):
            return nc.vector.scalar_tensor_tensor(dest[:, k, :], h[:, k, :], omg[:, g.at % 4, k:k + 1], xr[:, k, :],
                                                  ALU.mult, ALU.add)

        def over_rows(v, n=G):
            return v[:, :].unsqueeze(1).to_broadcast([P, n, H])

        def by_std(t, prod, slot, at, row, n=G):
            for k in range(n):
                last = nc.vector.scalar_tensor_tensor(t[:, k, :], prod[:, k, 0:H], rs[:, slot, at + k:at + k + 1],
                                                      row[:, :], ALU.mult, ALU.mult)
            return last

        def beta(dve, d, g, t, by, n=G, name="beta", after="gamma"):
            d[after].after(dve, g)
            one_mark(d[name], dve, g, nc.vector.tensor_tensor(t, t, over_rows(by, n), ALU.add))

        def final(eng, vec, d, g, dest, n=G):
            d["relu"].after(eng, g)
            one_mark(d["final"], eng, g, vec.tensor_tensor(dest, dest, t_buf[:, g.at % 4, 0:n, :], ALU.add))

        block = ctx.enter_context(nc.Block())

        @block.sync
        def _(sp):
            sp.wait_ge(s_memset, 1)
            for dest, a in ((src_i, src), (dst_i, dst), (w_f, edge_weight)):
                sp.dma_start(dest[0:FULL, :], a[0:FULL * J].rearrange("(p j) -> p j", j=J)).then_inc(s_e, 16)
                sp.dma_start(dest[FULL:FULL + 1, 0:REST], a[FULL * J:E].rearrange("(p j) -> p j", p=1)).then_inc(s_e, 16)
            sp.dma_start(w_all[:, 0:2, :], msg_w.rearrange("(a p) h -> p a h", p=P)).then_inc(s_w, 16)
            sp.dma_start(w_all[:, 2:4, :], upd_w.rearrange("(a p) h -> p a h", p=P)).then_inc(s_w, 16)
            sp.dma_start(w_u1[:, H:H + 1], gate_w).then_inc(s_w, 16)
            sp.dma_start(bias[0:1, 0, 0:H], msg_b.rearrange("(a h) -> a h", a=1)).then_inc(s_w, 16)
            sp.dma_start(bias[0:1, 0, H:2 * H], upd_b.rearrange("(a h) -> a h", a=1)).then_inc(s_w, 16)
            sp.dma_start(bias[0:1, 0, 2 * H:2 * H + 1], gate_b.rearrange("(a h) -> a h", a=1)).then_inc(s_w, 16)
            for dest, a in ((g_msg, msg_g), (be_msg, msg_beta), (g_upd, upd_g), (be_upd, upd_beta)):
                sp.dma_start(dest[:, :], a.partition_broadcast(P)).then_inc(s_w, 16)
            sp.wait_ge(s_bsplit, 1)
            sp.dma_start(bias3[:, :], bias_b[0:1, :, :]).then_inc(s_b3, 16)

            def base(g):
                return LAST_BASE if g.turn is None and g.at == NG - 1 else g.times(P * G)

            def rows(t, g):
                b = base(g)
                v = t[b:b + P * G, :] if g.turn is None else t[bass.ds(b, P * G), :]
                return v.rearrange("(p k) h -> p k h", k=G)

            def node_step(s):
                if live(s, NG):
                    if beyond(s, XS):
                        nd["mix"].after(sp, s.back(XS))
                    sp.dma_start(xload[:, s.at % XS], rows(x, s)).then_inc(s_x[s.at % XS], 16)
                g = s.back(XS)
                if live(g, NG):
                    nd["final"].after(sp, g)
                    if g.turn is None and g.at == NG - 1:
                        q = g.back(1)
                        sp.wait_ge(s_st[q.at % 4], q.rounds(16, 16))
                    sp.dma_start(rows(out, g), o[:, g.at % 4]).then_inc(s_st[g.at % 4], 16)

            run_steps(sp, node_step, NG, XS, 9, 8)

            sums_v = sums_dram.rearrange("(p j) h -> p j h", j=J)

            def edge_step(g):
                ed["sum"].after(sp, g)
                c = g.times(G)
                v = sums_v[:, c:c + G, :] if g.turn is None else sums_v[:, bass.ds(c, G), :]
                sp.dma_start(v, acc[:, g.at % 4]).then_inc(s_sums[g.at % 4], 16)

            run_steps(sp, edge_step, EG, 0, 9, 4)
            for i in range(4):
                sp.wait_ge(s_st[i], 16 * len(range(i, NG, 4)))
                sp.wait_ge(s_sums[i], 16 * len(range(i, EG, 4)))
                sp.wait_ge(s_scat[i], 16 * G * len(range(i, EG, 4)))
            sp.wait_ge(s_to, 16)

        @block.gpsimd
        def _(pool):
            nc.gpsimd.memset(ones[:, :], 1.0)
            nc.gpsimd.memset(eps_col[:, :], EPS)
            nc.gpsimd.memset(ones3[:, :], 1.0)
            nc.gpsimd.iota(tidx[:, 2:3], [[0, 1]], base=0, channel_multiplier=J).then_inc(s_const, 1)
            pool.wait_ge(s_const, 1)
            nc.gpsimd.affine_select(out=ident[:, :], in_=ones[:, :], compare_op=ALU.is_equal, fill=0.0, base=0,
                                    pattern=[[1, P]], channel_multiplier=-1)
            nc.gpsimd.affine_select(out=below[:, :], in_=ones[:, :], compare_op=ALU.is_gt, fill=0.0, base=0,
                                    pattern=[[1, P]], channel_multiplier=-1)
            nc.gpsimd.affine_select(out=above[:, :], in_=ones[:, :], compare_op=ALU.is_gt, fill=0.0, base=0,
                                    pattern=[[-1, P]], channel_multiplier=1).then_inc(s_const, 1)

            pool.wait_ge(s_prep, FLAG)
            unordered = pool.value_load(flag_i[0:1, 0:1], min_val=0, max_val=1)
            with pool.If(unordered > 0):
                pool.dma_start(keys_i[:, 0:E], dst.partition_broadcast(P)).then_inc(s_key, 16)
                pool.wait_ge(s_rank, 1)
                last_row = pool.to_reg(EPAD - 1)
                with pool.Fori(0, J) as t:
                    nc.gpsimd.tensor_copy(stage_r[:, :], rank_i[:, bass.ds(t, 1)])
                    nc.gpsimd.tensor_copy(stage_e[:, :], rec[:, bass.ds(t * 4, 4)]).then_inc(s_stage, 1)
                    pool.wait_ge(s_stage, t + 1)
                    pool.reg_alu(last_row, last_row, EPAD - 1, ALU.min)
                    pool.indirect_dma_start(
                        out=sorted_dram, out_offset=bass.IndirectOffsetOnAxis(ap=stage_r[:, 0:1], axis=0),
                        in_=stage_e[:, :], in_offset=None, bounds_check=last_row, oob_is_err=False,
                    ).then_inc(s_row, 16)
                    pool.wait_ge(s_row, t * 16 + 16)
                pool.dma_start(rec[:, :], sorted_dram.rearrange("(p j) c -> p (j c)", j=J)).then_inc(s_back, 16)
                pool.wait_ge(s_back, 16)
            with pool.Else():
                pool.nop()

            pool.wait_ge(s_prep, INDICES)
            if_tail = dict(bounds_check=N - 1, oob_is_err=False)

            def gather(dest, rows, idx, s):
                pool.indirect_dma_start(out=dest, out_offset=None, in_=rows,
                                        in_offset=bass.IndirectOffsetOnAxis(ap=idx, axis=0),
                                        **(if_tail if rows is x else {})).then_inc(s, 16)

            def scatter(rows, idx, s):
                pool.indirect_dma_start(out=out, out_offset=bass.IndirectOffsetOnAxis(ap=idx, axis=0),
                                        in_=rows, in_offset=None, **if_tail).then_inc(s, 16)

            def gather_row(g, n):
                if n == 0 and g >= 4:
                    pool.wait_ge(s_gath[g % 4], 2 * G * 16 * (g // 4))
                c = g * G + n % G
                gather(slot(Group(g), n // G)[:, n % G, :], x, (gidx if n >= G else src_i)[:, c:c + 1], s_gath[g % 4])

            def gather_group(g):
                for n in range(2 * G):
                    gather_row(g, n)

            done = 0
            for g in range(NG):
                upto = min(RING * 2 * G, (g + 4) * RING * 2 * G // NG)
                for n in range(done, upto):
                    gather_row(n // (2 * G), n % (2 * G))
                done = upto
                final(pool, nc.gpsimd, nd, Group(g), o[:, g % 4])
            for i in range(4):
                pool.wait_ge(s_st[i], 16 * len(range(i, NG, 4)))
            for g in range(EG):
                pool.wait_ge(ed["final"].sem, g + 1)
                for k in range(G):
                    c = g * G + k
                    scatter(o[:, g % 4, k, :], sidx[:, c:c + 1], s_scat[g % 4])
                if g + RING < EG:
                    gather_group(g + RING)
                if g == TAIL_SLOT:
                    gather(tail_x, x, tidx[:, 0:1], s_tx)
            for i in range(4):
                pool.wait_ge(s_sums[i], 16 * len(range(i, EG, 4)))
            gather(tail_f, sums_dram, tidx[:, 2:3], s_tf)
            pool.wait_ge(tl["final"].sem, 1)
            scatter(tail_o, tidx[:, 1:2], s_to)
            pool.wait_ge(s_to, 16)

        @block.vector
        def _(dve):
            prep_n = [0]

            def link(ins):
                prep_n[0] += 1
                ins.then_inc(s_prep, 1)
                dve.wait_ge(s_prep, prep_n[0])

            nc.vector.memset(src_i[:, :], 0)
            nc.vector.memset(dst_i[:, :], NO_NODE)
            nc.vector.memset(w_f[:, :], 0.0).then_inc(s_memset, 1)
            nc.vector.memset(cont[:, :], 0.0)
            nc.vector.memset(mv[:, :, :, :], 1.0)
            link(nc.vector.memset(ones_j, 1.0))
            dve.wait_ge(s_e, 6 * 16)
            dve.wait_ge(s_const, 2)

            def border_columns():
                link(nc.vector.tensor_copy(dst_f, dst_i[:, :]))
                nc.vector.tensor_scalar(dbf, ones[:, :], dst_f[:, 0:1], None, ALU.mult)
                link(nc.vector.tensor_scalar(dbl, ones[:, :], dst_f[:, J - 1:J], None, ALU.mult))

            border_columns()
            assert prep_n[0] == BORDERS1, prep_n
            nc.vector.tensor_tensor(viol[:, 0:J - 1], dst_f[:, 0:J - 1], dst_f[:, 1:J], ALU.is_gt)
            link(nc.vector.memset(viol[:, J - 1:J], 0.0))
            link(nc.vector.reduce_sum(col[:, 0:1], viol, AX.X))
            dve.wait_ge(s_prep_pe, 1)
            link(nc.vector.scalar_tensor_tensor(scr, pm[:, 0, :], dst_f[:, J - 1:J], below[:, :],
                                                ALU.is_lt, ALU.mult, accum_out=col[:, 1:2]))
            link(nc.vector.tensor_tensor(col[:, 2:3], col[:, 0:1], col[:, 1:2], ALU.add))
            assert prep_n[0] == VIOLATIONS, prep_n
            dve.wait_ge(s_prep_pe, 2)
            link(nc.vector.tensor_scalar(flag_i[0:1, 0:1], pm[0:1, 2, 0:1], 1.0, None, ALU.min))
            assert prep_n[0] == FLAG, prep_n
            unordered = dve.value_load(flag_i[0:1, 0:1], min_val=0, max_val=1)
            with dve.If(unordered > 0):
                fall = [0]

                def flink(ins, n=None):
                    fall[0] += 1
                    ins.then_inc(s_fall, 1)
                    dve.wait_ge(s_fall, fall[0] if n is None else n)

                nc.vector.memset(keys[:, E:EPAD], float(NO_NODE))
                nc.vector.memset(rec[:, :], 0)
                dve.wait_ge(s_key, 16)
                flink(nc.vector.tensor_copy(keys[:, 0:E], keys_i[:, 0:E]))
                key_cols = keys[:, :].rearrange("p (q j) -> p q j", j=J)
                half = EPAD // 2
                with dve.Fori(0, J) as t:
                    d = dst_f[:, bass.ds(t, 1)]
                    for m in range(2):
                        nc.vector.tensor_scalar(smaller[:, m * half:(m + 1) * half], keys[:, m * half:(m + 1) * half], d, None,
                                                ALU.is_lt, ALU.add, accum_out=col[:, 4 + m:5 + m])
                    nc.vector.scalar_tensor_tensor(scr, key_cols[:, :, bass.ds(t, 1)].rearrange("p q a -> p (q a)"), d,
                                                   above[:, :], ALU.is_equal, ALU.mult,
                                                   accum_out=col[:, 6:7]).then_inc(s_fall, 1)
                    dve.wait_ge(s_fall, t * 3 + 2)
                    nc.vector.tensor_scalar(key_cols[:, :, bass.ds(t, 1)], key_cols[:, :, bass.ds(t, 1)], 0.5, None,
                                            ALU.subtract)
                    nc.vector.tensor_tensor(col[:, 7:8], col[:, 4:5], col[:, 5:6], ALU.add).then_inc(s_fall, 1)
                    dve.wait_ge(s_fall, t * 3 + 3)
                    nc.vector.tensor_tensor(rank_i[:, bass.ds(t, 1)], col[:, 7:8], col[:, 6:7],
                                            ALU.add).then_inc(s_fall, 1)
                    dve.wait_ge(s_fall, t * 3 + 4)
                rec_v = rec[:, :].rearrange("p (j c) -> p j c", c=4)
                nc.vector.tensor_copy(rec_v[:, :, 0], src_i[:, :])
                nc.vector.tensor_copy(rec_v[:, :, 1], dst_i[:, :])
                nc.vector.tensor_copy(rec_v[:, :, 2].bitcast(f32), w_f[:, :]).then_inc(s_rank, 1)
                dve.wait_ge(s_back, 16)
                nc.vector.tensor_copy(src_i[:, :], rec_v[:, :, 0])
                nc.vector.tensor_copy(dst_i[:, :], rec_v[:, :, 1])
                nc.vector.tensor_copy(w_f[:, :], rec_v[:, :, 2].bitcast(f32)).then_inc(s_rank, 1)
                dve.wait_ge(s_rank, 2)
            with dve.Else():
                nc.vector.memset(col[:, 8:9], 0.0)

            border_columns()
            assert prep_n[0] == BORDERS2, prep_n
            link(nc.vector.tensor_tensor(cont[:, 1:J], dst_f[:, 1:J], dst_f[:, 0:J - 1], ALU.is_equal))
            nc.vector.tensor_tensor_scan(run_f, cont[:, 0:J], ones_j, 0.0, ALU.mult, ALU.add)
            nc.vector.tensor_tensor_scan(run_b[:, ::-1], cont[:, 1:J + 1][:, ::-1], ones_j, 0.0, ALU.mult, ALU.add)
            nc.vector.tensor_scalar(is_first, dst_f, dst_f[:, 0:1], None, ALU.is_equal)
            link(nc.vector.tensor_scalar(is_last, dst_f, dst_f[:, J - 1:J], None, ALU.is_equal))
            nc.vector.tensor_copy(col[:, 9:10], run_f[:, J - 1:J])
            link(nc.vector.reduce_sum(col[:, 10:11], is_first, AX.X))
            dve.wait_ge(s_prep_pe, 3)
            nc.vector.scalar_tensor_tensor(carry_m[:, :], pm[:, 0, :], dst_f[:, J - 1:J], below[:, :],
                                           ALU.is_equal, ALU.mult)
            link(nc.vector.scalar_tensor_tensor(m2, pm[:, 1, :], dst_f[:, 0:1], above[:, :],
                                                ALU.is_equal, ALU.mult))
            assert prep_n[0] == MATRICES, prep_n
            link(nc.vector.tensor_tensor(cnt, run_f, run_b, ALU.add))
            dve.wait_ge(s_prep_pe, 4)
            link(nc.vector.tensor_copy(col[:, 12:14], pm[:, 2, 0:2]))
            before_n, after_n = col[:, 12:13], col[:, 13:14]
            link(nc.vector.scalar_tensor_tensor(cnt, is_first, before_n, cnt, ALU.mult, ALU.add))
            link(nc.vector.scalar_tensor_tensor(cnt, is_last, after_n, cnt, ALU.mult, ALU.add))
            link(nc.vector.tensor_scalar(cnt, cnt, -1.0, None, ALU.add))
            nc.vector.tensor_scalar(col[:, 14:15], before_n, 0.0, None, ALU.is_gt)
            nc.vector.tensor_scalar(col[:, 15:16], after_n, 0.0, None, ALU.is_gt)
            link(nc.vector.reciprocal(wb[:, :], cnt))
            nc.vector.tensor_scalar(col[:, 16:17], col[:, 10:11], float(J), None, ALU.is_equal)
            nc.vector.tensor_tensor(wb[:, :], wb[:, :], w_f[:, :], ALU.mult)
            nc.vector.tensor_scalar(ok[:, 0:J - 1], cont[:, 1:J], -1.0, 1.0, ALU.mult, ALU.add)
            nc.vector.tensor_scalar(ok[:, J - 1:J], col[:, 15:16], -1.0, 1.0, ALU.mult, ALU.add)
            link(nc.vector.tensor_scalar(is_first, is_first, col[:, 14:15], None, ALU.mult))
            nc.vector.tensor_tensor(col[:, 17:18], col[:, 16:17], col[:, 15:16], ALU.mult)
            link(nc.vector.tensor_scalar(is_first, is_first, -1.0, 1.0, ALU.mult, ALU.add))
            nc.vector.tensor_scalar(col[:, 18:19], col[:, 17:18], -1.0, 1.0, ALU.mult, ALU.add)
            link(nc.vector.tensor_tensor(ok, ok, is_first, ALU.mult))
            nc.vector.tensor_tensor(col[:, 19:20], col[:, 18:19], col[:, 14:15], ALU.mult)
            link(nc.vector.scalar_tensor_tensor(ok, dst_f, float(N), ok, ALU.is_lt, ALU.mult))
            nc.vector.tensor_scalar(col[:, 20:21], col[:, 19:20], -FAR, FAR, ALU.mult, ALU.add)
            link(nc.vector.tensor_scalar(ok, ok, -FAR, FAR, ALU.mult, ALU.add))
            nc.vector.tensor_tensor(sidx[:, :], dst_f, ok, ALU.add)
            nc.vector.tensor_tensor(tidx[:, 1:2], dst_f[:, 0:1], col[:, 20:21], ALU.add)
            nc.vector.tensor_copy(tidx[:, 0:1], dst_f[:, 0:1])
            nc.vector.scalar_tensor_tensor(tidx[:, 2:3], col[:, 10:11], -1.0, tidx[:, 2:3], ALU.add, ALU.add)
            link(nc.vector.tensor_scalar(gidx[:, :], dst_f, float(N - 1), None, ALU.min))
            assert prep_n[0] == INDICES, prep_n

            dve.wait_ge(s_w, 10 * 16)
            nc.vector.reduce_sum(bias_sum[0:1, 0:2], bias[0:1, 0, 0:2 * H].rearrange("p (a h) -> p a h", a=2), AX.X)
            link(nc.vector.reduce_sum(wmean[:, :], w_all[:, :, :], AX.X))
            nc.vector.tensor_scalar(bias_sum[0:1, :], bias_sum[0:1, :], 1.0 / H, None, ALU.mult)
            link(nc.vector.tensor_scalar(wmean[:, :], wmean[:, :], 1.0 / H, None, ALU.mult))
            for a in range(4):
                nc.vector.tensor_scalar(w_all[:, a, :], w_all[:, a, :], wmean[:, a:a + 1], None, ALU.subtract)
            for a in range(2):
                last = nc.vector.tensor_scalar(bias[0:1, 0, a * H:(a + 1) * H], bias[0:1, 0, a * H:(a + 1) * H],
                                               bias_sum[0:1, a:a + 1], None, ALU.subtract)
            link(last)
            nc.vector.tensor_copy(w_u1[:, 0:H], w_all[:, 2, :])
            link(nc.vector.tensor_copy(bias_b[0:1, 0, :], bias[0:1, 0, :]))
            link(nc.vector.tensor_tensor(bias[0:1, 1, :], bias[0:1, 0, :], bias_b[0:1, 0, :], ALU.subtract))
            link(nc.vector.tensor_copy(bias_b[0:1, 1, :], bias[0:1, 1, :]))
            link(nc.vector.tensor_tensor(bias[0:1, 2, :], bias[0:1, 1, :], bias_b[0:1, 1, :], ALU.subtract))
            nc.vector.tensor_copy(bias_b[0:1, 2, :], bias[0:1, 2, :]).then_inc(s_bsplit, 1)
            dve.wait_ge(s_bsplit, 1)
            assert prep_n[0] == WEIGHTS, prep_n

            def node_step(s):
                g = s.back(4)
                fin, new = live(g, NG), live(s, NG)
                if fin:
                    gain(dve, nd, g, 0)
                if new:
                    dve.wait_ge(s_x[s.at % XS], s.rounds(16, 16, XS))
                    L = nd["stats"]
                    row_stats(L, s, xload[:, s.at % XS, 0:1], 0)
                if fin:
                    gain(dve, nd, g, 1)
                if new:
                    row_stats(L, s, xload[:, s.at % XS, 1:2], 1)
                if fin:
                    gain(dve, nd, g, 2)
                if new:
                    L.begin(dve, s)
                    L.mark(row_stats(L, s, xload[:, s.at % XS, 2:4], 2))
                    L.wait()
                if live(s.back(1), NG):
                    minus_mean(dve, nd, s.back(1), G)
                if new:
                    aggregate(L, s, G)
                if fin:
                    if beyond(g, 4):
                        dve.wait_ge(s_st[g.at % 4], g.rounds(16))
                    nd["rstd"].after(dve, s)
                    one_mark(nd["gamma"], dve, g, by_std(t_buf[:, g.at % 4], py[:, g.at % 2], s.at % 4, G, g_upd))
                    nd["gain"].after(dve, g)
                    for k in range(G):
                        last = mix_row(g, k, hrow[:, g.at % 4], xload[:, g.at % XS], o[:, g.at % 4])
                    one_mark(nd["mix"], dve, g, last)
                    beta(dve, nd, g, t_buf[:, g.at % 4], be_upd)

            run_steps(dve, node_step, NG, 5, 9, 8)

            nc.vector.memset(acc[:, 3, G - 1, :], 0.0).then_inc(s_bsplit, 1)
            dve.wait_ge(s_bsplit, 2)
            for i in range(4):
                dve.wait_ge(s_st[i], 16 * len(range(i, NG, 4)))

            def edge_step(s):
                g, m = s.back(6), s.back(4)
                fin, new, summing = live(g, EG), live(s, EG), live(m, EG)
                if fin:
                    gain(dve, ed, g, 0)
                if new:
                    dve.wait_ge(s_gath[s.at % 4], s.rounds(2 * G * 16, 2 * G * 16))
                    at = slot_base(dve, s)
                    L = ed["stats"]
                    row_stats(L, s, slot(s, 0, at)[:, 0:2], 0)
                if fin:
                    gain(dve, ed, g, 1)
                if new:
                    row_stats(L, s, slot(s, 0, at)[:, 2:4], 2)
                if fin:
                    gain(dve, ed, g, 2)
                if live(s.back(1), EG):
                    minus_mean(dve, ed, s.back(1), 2 * G)
                q = s.back(3)
                if live(q, EG):
                    if beyond(q, 4):
                        dve.wait_ge(s_sums[q.at % 4], q.rounds(16))
                    ed["rstd"].after(dve, s)
                    one_mark(ed["gamma_m"], dve, q, by_std(acc[:, q.at % 4], pm, s.at % 4, 2 * G, g_msg))
                if new:
                    L.begin(dve, s)
                    L.mark(row_stats(L, s, slot(s, 1, at), G))
                if fin:
                    if beyond(g, 4):
                        dve.wait_ge(s_scat[g.at % 4], g.rounds(16 * G))
                    ed["gain"].after(dve, g)
                    fat = slot_base(dve, g)
                if summing:
                    ed["msgw"].after(dve, m)
                    c = m.times(G) if m.turn is None else dve.snap(m.times(G))
                    before = acc[:, (m.at - 1) % 4, G - 1, :]
                    S = ed["sum"]
                    S.begin(dve, m)
                for k in range(G):
                    if summing:
                        if k:
                            S.wait()
                        S.mark(nc.vector.scalar_tensor_tensor(acc[:, m.at % 4, k, :], before, column(cont, c, k),
                                                              acc[:, m.at % 4, k, :], ALU.mult, ALU.add))
                        before = acc[:, m.at % 4, k, :]
                    if fin:
                        last = mix_row(g, k, h_dst[:, g.at % XS], slot(g, 1, fat), o[:, g.at % 4])
                if fin:
                    one_mark(ed["mix"], dve, g, last)
                if new:
                    L.wait()
                if fin:
                    ed["rstd"].after(dve, s)
                    one_mark(ed["gamma"], dve, g, by_std(t_buf[:, g.at % 4], py[:, g.at % 2], s.at % 4, 3 * G, g_upd))
                if new:
                    aggregate(L, s, 2 * G)
                if live(q, EG):
                    beta(dve, ed, q, acc[:, q.at % 4], be_msg, G, "beta_m", "gamma_m")
                if live(s.back(7), EG):
                    final(dve, nc.vector, ed, s.back(7), o[:, (s.at - 7) % 4])
                if fin:
                    beta(dve, ed, g, t_buf[:, g.at % 4], be_upd)
                if live(q, EG):
                    c = q.times(G)
                    weights = wb[:, c:c + G] if q.turn is None else wb[:, bass.ds(dve.snap(c), G)]
                    ed["beta_m"].after(dve, q)
                    one_mark(ed["msgw"], dve, q, nc.vector.scalar_tensor_tensor(
                        acc[:, q.at % 4], acc[:, q.at % 4], 0.0, weights.unsqueeze(2).to_broadcast([P, G, H]),
                        ALU.max, ALU.mult))

            run_steps(dve, edge_step, EG, 7, 9, 8)

            z = Group(0)
            dve.wait_ge(s_tx, 16)
            tx, th = tail_x.unsqueeze(1), tail_h.unsqueeze(1)
            L = tl["stats"]
            L.begin(dve, z)
            L.mark(row_stats(L, z, tx, 0))
            L.wait()
            aggregate(L, z, 1)
            tl["rstd"].after(dve, z)
            one_mark(tl["nb"], dve, z, nc.vector.scalar_tensor_tensor(
                nb[:, 1, 0:1], mv[:, 1, 0:1, 0], -1.0, rs[:, 1, 0:1], ALU.mult, ALU.mult))
            tl["msg"].after(dve, z)
            dve.wait_ge(s_tf, 16)
            one_mark(tl["sum"], dve, z, nc.vector.tensor_tensor(tail_a, pm[:, 0, :], tail_f, ALU.add))
            for k in range(3):
                gain(dve, tl, z, k, 1)
            tl["gain"].after(dve, z)
            one_mark(tl["mix"], dve, z, mix_row(z, 0, th, tx, tail_o.unsqueeze(1)))
            dve.wait_ge(tl["rstd"].sem, 2)
            one_mark(tl["gamma"], dve, z, by_std(t_buf[:, 0], py[:, 0], 2, 0, g_upd, 1))
            beta(dve, tl, z, t_buf[:, 0, 0:1], be_upd, 1)
            final(dve, nc.vector, tl, z, tail_o.unsqueeze(1), 1)

        @block.scalar
        def _(act):
            nc.scalar.preload_act_table_set("natural_log_exp_and_others")
            act.wait_ge(s_prep, WEIGHTS)

            def evacuate(d, g, dest, source, func, stage, flip):
                d[flip].after(act, g)
                one_mark(d[stage], act, g, nc.scalar.activation(dest, source, func))

            def node_step(s):
                if live(s.back(1), NG):
                    nd["stats"].after(act, s.back(1))
                if live(s.back(4), NG):
                    nd["post"].after(act, s.back(4))
                logs(act, nd, s, 2 * G)
                if live(s.back(5), NG):
                    gated_relu(act, nd, s.back(5))
                rstds(act, nd, s, 2 * G)
                g = s.back(2)
                if live(g, NG):
                    evacuate(nd, g, ht_dst[:, g.at % 4, :], pt[:, g.at % 2, :], ACT.Copy, "ht", "flip")
                if live(s.back(3), NG):
                    post(act, nd, s.back(3), (s.at + 1) % 4, G)
                g = s.back(1)
                if live(g, NG):
                    nd["nb"].after(act, g)
                    one_mark(nd["h"], act, g, h_rows(g, hrow[:, g.at % 4], xload[:, g.at % XS], 0))

            run_steps(act, node_step, NG, 5, 9, 8)

            def edge_step(s):
                if live(s.back(1), EG):
                    ed["stats"].after(act, s.back(1))
                if live(s.back(6), EG):
                    ed["post"].after(act, s.back(6))
                if live(s.back(3), EG):
                    ed["square_m"].after(act, s.back(3))
                logs(act, ed, s, 4 * G)
                g = s.back(2)
                if live(g, EG):
                    ed["flip"].after(act, g)
                    nc.scalar.activation(ht_src[:, g.at % 2, :], pt[:, 0, :], ACT.Copy)
                rstds(act, ed, s, 4 * G)
                if live(g, EG):
                    one_mark(ed["ht"], act, g, nc.scalar.activation(ht_dst[:, g.at % 4, :], pt[:, 1, :], ACT.Copy))
                if live(s.back(7), EG):
                    gated_relu(act, ed, s.back(7))
                if live(s.back(5), EG):
                    post(act, ed, s.back(5), (s.at + 1) % 4, 3 * G)
                g = s.back(1)
                if live(g, EG):
                    ed["nb"].after(act, g)
                    at = slot_base(act, g)
                    H_ = ed["h"]
                    H_.begin(act, g)
                    H_.mark(h_rows(g, hrow[:, g.at % 4], slot(g, 0, at), 0))
                if live(g, EG):
                    H_.mark(h_rows(g, h_dst[:, g.at % XS], slot(g, 1, at), G))
                g = s.back(4)
                if live(g, EG):
                    evacuate(ed, g, at_[:, g.at % 2, :], pa[:, :], ACT.Copy, "at", "aflip")
                if live(s.back(2), EG):
                    ed["msg"].after(act, s.back(2))
                    one_mark(ed["square_m"], act, s.back(2), squares(pm, (s.at + 1) % 4, 2 * G, G, 1))

            run_steps(act, edge_step, EG, 7, 9, 8)

            z = Group(0)
            tl["stats"].after(act, z)
            one_mark(tl["ln"], act, z, nc.scalar.activation(lnv[:, 1, 0:1], mv[:, 1, 0:1, 1], ACT.Ln, bias=eps_col[:, :]))
            tl["ln"].after(act, z)
            one_mark(tl["rstd"], act, z, nc.scalar.activation(rs[:, 1, 0:1], lnv[:, 1, 0:1], ACT.Exp, scale=-0.5))
            tl["nb"].after(act, z)
            one_mark(tl["h"], act, z, h_rows(z, tail_h.unsqueeze(1), tail_x.unsqueeze(1), 0))
            evacuate(tl, z, ht_dst[:, 0, 0:H], pt[:, 0, 0:H], ACT.Copy, "ht", "flip")
            evacuate(tl, z, at_[:, 1, 0:H], pa[:, 0:H], ACT.Copy, "at", "aflip")
            post(act, tl, z, 2, 0, 1)
            tl["post"].after(act, z)
            nc.scalar.activation(lnv[:, 2, 0:1], mv[:, 2, 0:1, 1], ACT.Ln, bias=eps_col[:, :]).then_inc(tl["ln"].sem, 1)
            act.wait_ge(tl["ln"].sem, 2)
            nc.scalar.activation(rs[:, 2, 0:1], lnv[:, 2, 0:1], ACT.Exp, scale=-0.5).then_inc(tl["rstd"].sem, 1)
            gated_relu(act, tl, z, 1)

        @block.tensor
        def _(pe):
            def flip(dest, rows):
                for k in range(rows.shape[1]):
                    last = nc.tensor.transpose(dest[:, k * H:(k + 1) * H], rows[:, k, :], ident[:, :])
                return last

            def put_bias(dest, lo, hi):
                n = dest.shape[1]
                nc.tensor.matmul(dest, ones3[:, :], bias3[:, lo:hi].unsqueeze(1).to_broadcast([3, n, hi - lo]),
                                 start=True, stop=False)

            def spread(dest, column_spread):
                return nc.tensor.matmul(dest, column_spread, ident[:, :], start=True, stop=True)

            pe.wait_ge(s_const, 2)
            pe.wait_ge(s_prep, BORDERS1)
            spread(pm[:, 0, :], dbf).then_inc(s_prep_pe, 1)
            pe.wait_ge(s_prep, VIOLATIONS)
            nc.tensor.matmul(pm[0:1, 2, 0:1], col[:, 2:3], ones[:, 0:1], start=True, stop=True).then_inc(s_prep_pe, 1)
            pe.wait_ge(s_prep, BORDERS2)
            spread(pm[:, 0, :], dbf)
            spread(pm[:, 1, :], dbl).then_inc(s_prep_pe, 1)
            pe.wait_ge(s_prep, MATRICES)
            nc.tensor.matmul(pm[:, 2, 0:1], carry_m[:, :], col[:, 9:10], start=True, stop=True)
            nc.tensor.matmul(pm[:, 2, 1:2], m2, col[:, 10:11], start=True, stop=True).then_inc(s_prep_pe, 1)
            pe.wait_ge(s_b3, 16)
            pe.wait_ge(s_prep, WEIGHTS)

            def node_step(s):
                g = s.back(2)
                if live(g, NG):
                    nd["ht"].after(pe, g)
                    if beyond(g, 2):
                        nd["gamma"].after(pe, g.back(2))
                    for k in range(0, G, 2):
                        put_bias(py[:, g.at % 2, k:k + 2, 0:H + 1], H, 2 * H + 1)
                    for k in range(G):
                        last = nc.tensor.matmul(py[:, g.at % 2, k, 0:H + 1], ht_dst[:, g.at % 4, k * H:(k + 1) * H],
                                                w_u1[:, :], start=False, stop=k % 2 == 1)
                    one_mark(nd["upd"], pe, g, last)
                g = s.back(1)
                if live(g, NG):
                    nd["h"].after(pe, g)
                    one_mark(nd["flip"], pe, g, flip(pt[:, g.at % 2, :], hrow[:, g.at % 4]))

            run_steps(pe, node_step, NG, 2, 9, 8)

            def edge_step(s):
                g = s.back(2)
                if live(g, EG):
                    ed["ht"].after(pe, g)
                    if beyond(g, 1):
                        ed["gamma_m"].after(pe, g.back(1))
                    put_bias(pm[:, :, :], 0, H)
                    for k in range(G):
                        nc.tensor.matmul(pm[:, k, :], ht_src[:, g.at % 2, k * H:(k + 1) * H], w_all[:, 0, :],
                                         start=False, stop=False)
                        last = nc.tensor.matmul(pm[:, k, :], ht_dst[:, g.at % 4, k * H:(k + 1) * H], w_all[:, 1, :],
                                                start=False, stop=k == G - 1)
                    one_mark(ed["msg"], pe, g, last)
                g = s.back(4)
                if live(g, EG):
                    ed["sum"].after(pe, g)
                    one_mark(ed["aflip"], pe, g, flip(pa[:, :], acc[:, g.at % 4]))
                g = s.back(1)
                if live(g, EG):
                    ed["h"].after(pe, g)
                    flip(pt[:, 0, :], hrow[:, g.at % 4])
                    one_mark(ed["flip"], pe, g, flip(pt[:, 1, :], h_dst[:, g.at % XS]))
                g = s.back(4)
                if live(g, EG):
                    if beyond(g, 2):
                        ed["gamma"].after(pe, g.back(2))
                    else:
                        nd["gamma"].after(pe, Group(NG - 1))
                    ed["at"].after(pe, g)
                    for k in range(0, G, 2):
                        put_bias(py[:, g.at % 2, k:k + 2, 0:H + 1], H, 2 * H + 1)
                    for k in range(G):
                        nc.tensor.matmul(py[:, g.at % 2, k, 0:H], at_[:, g.at % 2, k * H:(k + 1) * H], w_all[:, 3, :],
                                         start=False, stop=False)
                        last = nc.tensor.matmul(py[:, g.at % 2, k, 0:H + 1], ht_dst[:, g.at % 4, k * H:(k + 1) * H],
                                                w_u1[:, :], start=False, stop=k % 2 == 1)
                    one_mark(ed["upd"], pe, g, last)

            run_steps(pe, edge_step, EG, 4, 9, 8)

            z = Group(0)
            nc.tensor.matmul(pm[:, 0, :], carry_m[:, :], acc[:, (EG - 1) % 4, G - 1, :], start=True, stop=True
                             ).then_inc(tl["msg"].sem, 1)
            tl["h"].after(pe, z)
            nc.tensor.transpose(pt[:, 0, 0:H], tail_h, ident[:, :]).then_inc(tl["flip"].sem, 1)
            pe.wait_ge(tl["sum"].sem, 1)
            nc.tensor.transpose(pa[:, 0:H], tail_a, ident[:, :]).then_inc(tl["aflip"].sem, 1)
            tl["ht"].after(pe, z)
            tl["at"].after(pe, z)
            put_bias(py[:, 0, 0:1, 0:H + 1], H, 2 * H + 1)
            nc.tensor.matmul(py[:, 0, 0, 0:H], at_[:, 1, 0:H], w_all[:, 3, :], start=False, stop=False)
            nc.tensor.matmul(py[:, 0, 0, 0:H + 1], ht_dst[:, 0, 0:H], w_u1[:, :], start=False, stop=True
                             ).then_inc(tl["upd"].sem, 1)


INPUTS = ["x", "src", "dst", "edge_weight"] + ["L0_gnn_" + n for n in (
    "msg_w", "msg_b", "msg_g", "msg_beta", "upd_w", "upd_b", "upd_g", "upd_beta", "gate_w", "gate_b")]


def kernel(**inputs):
    import numpy as np
    import concourse.bacc as bacc
    from concourse.bass_utils import run_bass_kernel_spmd

    nc = bacc.Bacc("TRN2", target_bir_lowering=False, num_devices=1)
    arrays, args = {}, []
    for name in INPUTS:
        a = np.ascontiguousarray(inputs[name])
        arrays[f"in_{name}"] = a
        args.append(nc.dram_tensor(f"in_{name}", a.shape, mybir.dt.from_np(a.dtype), kind="ExternalInput").ap())
    out = nc.dram_tensor("out", (N, H), f32, kind="ExternalOutput").ap()
    build(nc, *args, out)
    r = run_bass_kernel_spmd(nc, [arrays], core_ids=[0])
    return r.results[0]["out"]
```

```python
from contextlib import ExitStack

import concourse.bass as bass
from concourse import mybir

N, E, H = 50000, 25000, 128
P = 128
G = 4
NG = -(-N // (P * G))
LAST_BASE = N - P * G
J = 196
EG = J // G
EPAD = P * J
FULL = E // J
REST = E - FULL * J
RING = 32
REFILL = 3
EPS = 1e-5
FAR = float(1 << 20)
NO_NODE = 1 << 17
EUN = 8
XS = 8

BORDERS1, VIOLATIONS, FLAG, BORDERS2, MATRICES, WEIGHTS, INDICES = 3, 7, 8, 10, 14, 23, 33

f32, bf16, i32 = mybir.dt.float32, mybir.dt.bfloat16, mybir.dt.int32
u32, u8 = mybir.dt.uint32, mybir.dt.uint8
ALU, ACT, AX = mybir.AluOpType, mybir.ActivationFunctionType, mybir.AxisListType


class Group:

    def __init__(self, at, turn=None, un=0, bases=None):
        self.at, self.turn, self.un, self.bases = at, turn, un, bases

    def back(self, k):
        return Group(self.at - k, self.turn, self.un, self.bases)

    def times(self, c, d=0):
        return c * self.at + d if self.turn is None else self.turn * (c * self.un) + (c * self.at + d)

    def rounds(self, c, d=0, ring=4):
        a = c * (self.at // ring) + d
        return a if self.turn is None else self.turn * (c * self.un // ring) + a


class Steps:

    def __init__(self, sem, per):
        self.sem, self.per, self.eng, self.g, self.n = sem, per, None, None, 0

    def begin(self, eng, g):
        self.eng, self.g, self.n = eng, g, 0

    def mark(self, ins):
        self.n += 1
        assert self.n <= self.per
        ins.then_inc(self.sem, 1)

    def wait(self):
        self.eng.wait_ge(self.sem, self.g.times(self.per, self.n))

    def after(self, eng, g, n=None):
        eng.wait_ge(self.sem, g.times(self.per, self.per if n is None else n))


def run_steps(eng, step, n_groups, skew, lead, un, first=0, beside=None):
    turns = (n_groups - 1 - lead) // un
    stop = lead + turns * un
    for s in range(first, lead):
        step(Group(s))
    with eng.Fori(0, turns) as i:
        bases = {}
        for u in range(un):
            step(Group(lead + u, i, un, bases))
    for s in range(stop, n_groups + skew):
        step(Group(s))
        if beside is not None and s >= n_groups:
            beside(Group(s - n_groups))


def live(g, n_groups):
    return g.turn is not None or 0 <= g.at < n_groups


def beyond(g, n):
    return g.turn is not None or g.at >= n


def build(nc, x, src, dst, edge_weight, msg_w, msg_b, msg_g, msg_beta, upd_w, upd_b, upd_g, upd_beta,
          gate_w, gate_b, out):
    ctx = ExitStack()
    nc.disable_value_cache = True
    with ctx:
        def sb(name, shape, dt=f32):
            return ctx.enter_context(nc.sbuf_tensor(name, shape, dt))

        def sem(name):
            return ctx.enter_context(nc.semaphore(name))

        def sem4(name):
            return [sem(f"{name}{i}") for i in range(4)]

        sums_dram = nc.dram_tensor("running_sums", (EPAD, H), f32).ap()
        sorted_dram = nc.dram_tensor("sorted_edges", (EPAD, 4), i32).ap()

        ring = sb("ring", [P, RING * 2 * G * H])
        work = sb("work", [P, 14 * G * H])
        o = work[:, 0:4 * G * H].rearrange("p (a k h) -> p a k h", a=4, h=H)
        t_buf = work[:, 4 * G * H:8 * G * H].rearrange("p (a k h) -> p a k h", a=4, h=H)
        ht_dst = work[:, 8 * G * H:12 * G * H].rearrange("p (a f) -> p a f", a=4)
        ht_src = work[:, 12 * G * H:14 * G * H].rearrange("p (a f) -> p a f", a=2)
        hrow = sb("hrow", [P, 4, G, H])
        acc = sb("acc", [P, 4, G, H])
        at_ = sb("at", [P, 2, G * H])
        xload = sb("xload", [P, XS, G, H])
        junk = sb("junk", [P, 2, G, H], bf16)
        w_all = sb("w_all", [P, 4, H])
        w_u1 = sb("w_u1", [P, H + 1])
        g_msg = sb("g_msg", [P, H])
        be_msg = sb("be_msg", [P, H])
        g_upd = sb("g_upd", [P, H])
        be_upd = sb("be_upd", [P, H])
        ident = sb("ident", [P, P])
        ones = hrow[:, 0, 0, :]
        below = hrow[:, 0, 1, :]
        above = hrow[:, 0, 2, :]
        bias = hrow[0:1, 1:3, :, :].rearrange("p a b h -> p (a b h)")[:, 0:3 * (2 * H + 1)].rearrange(
            "p (c h) -> p c h", c=3)
        bias_sum = sb("bias_sum", [1, 2])
        bias_b = hrow[0:1, 3, :, :].rearrange("p b h -> p (b h)").bitcast(bf16)[:, 0:3 * (2 * H + 1)].rearrange(
            "p (c h) -> p c h", c=3)
        bias3 = sb("bias3", [3, 2 * H + 1], bf16)
        ones3 = sb("ones3", [3, P], bf16)
        wmean = sb("wmean", [P, 4])
        st = sb("st", [P, 4, 2 * G, 6])
        mv = sb("mv", [P, 4, 16, 2])
        lnv = sb("lnv", [P, 4, 16])
        rs = sb("rs", [P, 4, 16])
        s_dif = sb("s_dif", [P, 2 * G])
        s_var = sb("s_var", [P, 2 * G])
        tail_mv = sb("tail_mv", [P, 2, 2])
        tail_st = sb("tail_st", [P, 6])
        tail_ln = sb("tail_ln", [P, 2])
        tail_rs = sb("tail_rs", [P, 2])
        tail_nb = sb("tail_nb", [P, 1])
        nb = sb("nb", [P, 4, 2 * G])
        ge = sb("ge", [P, 2, G])
        e1 = sb("e1", [P, 4, G])
        gt = sb("gt", [P, 4, G])
        omg = sb("omg", [P, 4, G])
        src_i = sb("src_i", [P, J], i32)
        cont_wb = sb("cont_wb", [P, 2 * J])
        dst_i = cont_wb[:, 0:J].bitcast(i32)
        w_f = cont_wb[:, J:2 * J]
        cw = sb("cw", [P, 4, 2 * G])
        gidx = sb("gidx", [P, J], i32)
        sidx = sb("sidx", [P, J], i32)
        carry_m = sb("carry_m", [P, P])
        tidx = sb("tidx", [P, 3], i32)
        flag_i = sb("flag_i", [1, 1], i32)
        eps_col = sb("eps_col", [P, 1])
        prep = acc[:, :, :, :].rearrange("p a b c -> p (a b c)")

        def pre(i, n=J):
            return prep[:, i * (J + 4):i * (J + 4) + n]

        dst_f, ones_j, run_f, run_b, is_first, is_last, cnt, ok, viol = (pre(i) for i in range(9))
        cont = pre(9, J + 1)
        m2 = at_[:, 0, 0:P]
        dbf = at_[:, 0, P:2 * P]
        dbl = at_[:, 0, 2 * P:3 * P]
        scr = at_[:, 1, 0:P]
        col = at_[:, 1, P:P + 32]

        h_dst = xload

        TAIL_SLOT = EG - RING
        tail_x, tail_h, tail_f, tail_a, tail_o = (
            ring[:, (TAIL_SLOT * 2 * G + k) * H:(TAIL_SLOT * 2 * G + k + 1) * H] for k in range(5))

        keys = ring[:, 0:EPAD]
        keys_i = keys.bitcast(i32)
        smaller = work[:, 0:EPAD // 4].bitcast(u8)
        spare = ring[:, EPAD:EPAD + 5 * J + 8].bitcast(i32)
        rank_i = spare[:, 0:J]
        rec = spare[:, J:5 * J]
        stage_r, stage_e = spare[:, 5 * J:5 * J + 1], spare[:, 5 * J + 4:5 * J + 8]

        pt = ctx.enter_context(nc.psum_tensor("pt", [P, 2, G * H], f32))
        pm = ctx.enter_context(nc.psum_tensor("pm", [P, G, H], f32))
        pa = ctx.enter_context(nc.psum_tensor("pa", [P, G * H], f32))
        py = ctx.enter_context(nc.psum_tensor("py", [P, 2, G, 2 * H], f32))

        s_w = sem("weights_loaded")
        s_e = sem("edges_loaded")
        s_memset = sem("edge_pads_set")
        s_const = sem("constants_built")
        s_prep = sem("prep_done_by_vector")
        s_prep_pe = sem("prep_done_by_tensor")
        s_wready = sem("weights_centred")
        s_b3 = sem("bias_parts_placed")
        s_bsplit = sem("bias_parts_split")
        s_key = sem("sort_keys_loaded")
        s_rank = sem("edges_ranked")
        s_stage = sem("sort_row_staged")
        s_row = sem("sort_row_written")
        s_back = sem("sorted_edges_loaded")
        s_fall = sem("vector_steps_of_sort")
        s_x = [sem(f"x_loaded{i}") for i in range(XS)]
        s_st = sem4("node_rows_stored")
        s_gath = sem4("rows_gathered")
        s_scat = sem4("rows_scattered")
        s_sums = sem4("running_sums_stored")
        s_tx, s_tf, s_to = sem("tail_x_gathered"), sem("tail_sums_gathered"), sem("tail_scattered")

        def stages(kind, names):
            return {n: Steps(sem(f"{kind}_{n}"), per) for n, per in names.items()}

        common = {
            "stats": 2,
            "nb": 1,
            "gain": 3,
            "mix": 1,
            "gamma": 1, "beta": 1,
            "ln": 1, "rstd": 1,
            "h": 1,
            "ht": 1,
            "post": 1,
            "relu": 1,
            "relu_v": 1,
            "final": 1,
            "flip": 1,
            "upd": 1,
        }
        nd = stages("node", common)
        tl = stages("tail", common)
        tl.update(stages("tail", {"msg": 1, "sum": 1, "aflip": 1, "at": 1}))
        ed = stages("edge", {**common, "stats": 4, "h": 2, "ht": 1,
                             "gamma_m": 1, "beta_m": 1,
                             "cw": 1,
                             "msgw": 1,
                             "sum": G,
                             "square_m": 1,
                             "at": 1,
                             "msg": 1,
                             "aflip": 1})

        def rows4(v):
            return v.rearrange("p (k h) -> p k h", h=H)

        def slot(g, part, base=None, n=G):
            if g.turn is None:
                a = (g.at % RING) * 2 * G * H + part * G * H
                return rows4(ring[:, a:a + n * H])
            return rows4(ring[:, bass.ds(base + (g.at % EUN * 2 + part) * G * H, n * H)])

        def slot_base(eng, g):
            if g.turn is None:
                return None
            b = g.at // EUN
            if b not in g.bases:
                g.bases[b] = eng.snap(((g.turn + b) % (RING // EUN)) * (EUN * 2 * G * H))
            return g.bases[b]

        def one_mark(L, eng, g, ins):
            L.begin(eng, g)
            L.mark(ins)

        def row_stats(L, g, rows, at):
            for m in range(rows.shape[1]):
                last = nc.vector.bn_stats(st[:, g.at % 4, at + m, :], rows[:, m, :])
            return last

        def aggregate(L, g, n):
            for m in range(n):
                last = nc.vector.bn_aggr(mv[:, (g.at + 1) % 4, m, :], st[:, g.at % 4, m, :])
            L.mark(last)

        def moment(L, g, n, which):
            s4 = (g.at + 1) % 4
            v = st[:, g.at % 4, 0:n, :]
            if which == 0:
                nc.vector.tensor_tensor(mv[:, s4, 0:n, 0], v[:, :, 1], v[:, :, 4], ALU.add)
                nc.vector.tensor_tensor(s_dif[:, 0:n], v[:, :, 1], v[:, :, 4], ALU.subtract)
                L.mark(nc.vector.tensor_tensor(s_var[:, 0:n], v[:, :, 2], v[:, :, 5], ALU.add))
            elif which == 1:
                L.mark(nc.vector.tensor_tensor(s_dif[:, 0:n], s_dif[:, 0:n], s_dif[:, 0:n], ALU.mult))
            else:
                L.mark(nc.vector.scalar_tensor_tensor(mv[:, s4, 0:n, 1], s_dif[:, 0:n], H / 4, s_var[:, 0:n],
                                                      ALU.mult, ALU.add))

        def logs(act, d, s, k, scale=1.0):
            one_mark(d["ln"], act, s, nc.scalar.activation(lnv[:, s.at % 4, 0:k], mv[:, s.at % 4, 0:k, 1], ACT.Ln,
                                                           bias=eps_col[:, :], scale=scale))

        def rstds(act, d, s, k):
            act.wait_ge(d["ln"].sem, s.times(1, 1))
            one_mark(d["rstd"], act, s, nc.scalar.activation(rs[:, s.at % 4, 0:k], lnv[:, s.at % 4, 0:k], ACT.Exp,
                                                             scale=-0.5))

        def minus_mean(dve, d, g, n, factor=-1.0):
            d["rstd"].after(dve, g.back(-1))
            s4 = (g.at + 1) % 4
            one_mark(d["nb"], dve, g, nc.vector.scalar_tensor_tensor(
                nb[:, s4, 0:n], mv[:, s4, 0:n, 0], factor, rs[:, s4, 0:n], ALU.mult, ALU.mult))

        def h_rows(g, dest, rows, at):
            s4 = (g.at + 1) % 4
            for m in range(rows.shape[1]):
                last = nc.scalar.activation(dest[:, m, :], rows[:, m, :], ACT.Relu, bias=nb[:, s4, at + m:at + m + 1],
                                            scale=rs[:, s4, at + m:at + m + 1])
            return last

        def squares(prod, slot, at, n=G, j=0, scale=float(H) ** -0.5):
            for k in range(n):
                last = nc.scalar.activation(junk[:, j, k, :], prod[:, k, 0:H], ACT.Square, scale=scale,
                                            accum_out=mv[:, slot, at + k, 1:2])
            return last

        def post(act, d, g, slot, at, n=G, scale=float(H) ** -0.5):
            d["upd"].after(act, g)
            squares(py[:, g.at % 2], slot, at, n, 0, scale)
            one_mark(d["post"], act, g, nc.scalar.activation(ge[:, g.at % 2, 0:n], py[:, g.at % 2, 0:n, H], ACT.Exp,
                                                             scale=-1.0))

        def gated_relu(act, d, g, n=G, first=0, done=True):
            if first == 0:
                d["beta"].after(act, g)
            for k in range(first, n):
                last = nc.scalar.activation(t_buf[:, g.at % 4, k, :], t_buf[:, g.at % 4, k, :], ACT.Relu,
                                            scale=gt[:, g.at % 4, k:k + 1])
            if done:
                one_mark(d["relu"], act, g, last)

        def gain(dve, d, g, which, n=G):
            L, b = d["gain"], g.at % 4
            if which == 0:
                d["post"].after(dve, g)
                L.begin(dve, g)
                L.mark(nc.vector.tensor_scalar(e1[:, b, 0:n], ge[:, g.at % 2, 0:n], 1.0, None, ALU.add))
            elif which == 1:
                L.wait()
                L.mark(nc.vector.reciprocal(gt[:, b, 0:n], e1[:, b, 0:n]))
            else:
                L.wait()
                L.mark(nc.vector.tensor_scalar(omg[:, b, 0:n], gt[:, b, 0:n], -1.0, 1.0, ALU.mult, ALU.add))

        def mix_row(g, k, h, xr, dest):
            return nc.vector.scalar_tensor_tensor(dest[:, k, :], h[:, k, :], omg[:, g.at % 4, k:k + 1], xr[:, k, :],
                                                  ALU.mult, ALU.add)

        def over_rows(v, n=G):
            return v[:, :].unsqueeze(1).to_broadcast([P, n, H])

        def by_std(t, prod, slot, at, row, n=G, before_last=None):
            for k in range(n):
                if k == n - 1 and before_last is not None:
                    before_last()
                last = nc.vector.scalar_tensor_tensor(t[:, k, :], prod[:, k, 0:H], rs[:, slot, at + k:at + k + 1],
                                                      row[:, :], ALU.mult, ALU.mult)
            return last

        def beta(dve, d, g, t, by, n=G, name="beta", after="gamma"):
            d[after].after(dve, g)
            one_mark(d[name], dve, g, nc.vector.tensor_tensor(t, t, over_rows(by, n), ALU.add))

        def final(eng, vec, d, g, dest, n=G):
            d["relu"].after(eng, g)
            one_mark(d["final"], eng, g, vec.tensor_tensor(dest, dest, t_buf[:, g.at % 4, 0:n, :], ALU.add))

        block = ctx.enter_context(nc.Block())

        @block.sync
        def _(sp):
            sp.wait_ge(s_memset, 1)
            for dest, a in ((src_i, src), (dst_i, dst), (w_f, edge_weight)):
                sp.dma_start(dest[0:FULL, :], a[0:FULL * J].rearrange("(p j) -> p j", j=J)).then_inc(s_e, 16)
                sp.dma_start(dest[FULL:FULL + 1, 0:REST], a[FULL * J:E].rearrange("(p j) -> p j", p=1)).then_inc(s_e, 16)
            sp.dma_start(w_all[:, 0:2, :], msg_w.rearrange("(a p) h -> p a h", p=P)).then_inc(s_w, 16)
            sp.dma_start(w_all[:, 2:4, :], upd_w.rearrange("(a p) h -> p a h", p=P)).then_inc(s_w, 16)
            sp.dma_start(w_u1[:, H:H + 1], gate_w).then_inc(s_w, 16)
            sp.dma_start(bias[0:1, 0, 0:H], msg_b.rearrange("(a h) -> a h", a=1)).then_inc(s_w, 16)
            sp.dma_start(bias[0:1, 0, H:2 * H], upd_b.rearrange("(a h) -> a h", a=1)).then_inc(s_w, 16)
            sp.dma_start(bias[0:1, 0, 2 * H:2 * H + 1], gate_b.rearrange("(a h) -> a h", a=1)).then_inc(s_w, 16)
            for dest, a in ((g_msg, msg_g), (be_msg, msg_beta), (g_upd, upd_g), (be_upd, upd_beta)):
                sp.dma_start(dest[:, :], a.partition_broadcast(P)).then_inc(s_w, 16)

            def base(g):
                return LAST_BASE if g.turn is None and g.at == NG - 1 else g.times(P * G)

            def rows(t, g):
                b = base(g)
                v = t[b:b + P * G, :] if g.turn is None else t[bass.ds(b, P * G), :]
                return v.rearrange("(p k) h -> p k h", k=G)

            def node_step(s):
                if live(s, NG):
                    if beyond(s, XS):
                        nd["mix"].after(sp, s.back(XS))
                    sp.dma_start(xload[:, s.at % XS], rows(x, s)).then_inc(s_x[s.at % XS], 16)
                g = s.back(XS)
                if live(g, NG):
                    nd["final"].after(sp, g)
                    if g.turn is None and g.at == NG - 1:
                        q = g.back(1)
                        sp.wait_ge(s_st[q.at % 4], q.rounds(16, 16))
                    sp.dma_start(rows(out, g), o[:, g.at % 4]).then_inc(s_st[g.at % 4], 16)

            for g in range(XS):
                node_step(Group(g))
            sp.wait_ge(s_bsplit, 1)
            sp.dma_start(bias3[:, :], bias_b[0:1, :, :]).then_inc(s_b3, 16)
            run_steps(sp, node_step, NG, XS, 9, 8, first=XS)

            sums_v = sums_dram.rearrange("(p j) h -> p j h", j=J)

            def edge_step(g):
                ed["sum"].after(sp, g)
                c = g.times(G)
                v = sums_v[:, c:c + G, :] if g.turn is None else sums_v[:, bass.ds(c, G), :]
                sp.dma_start(v, acc[:, g.at % 4]).then_inc(s_sums[g.at % 4], 16)

            run_steps(sp, edge_step, EG, 0, 9, 4)
            for i in range(4):
                sp.wait_ge(s_st[i], 16 * len(range(i, NG, 4)))
                sp.wait_ge(s_sums[i], 16 * len(range(i, EG, 4)))
                sp.wait_ge(s_scat[i], 16 * G * len(range(i, EG, 4)))
            sp.wait_ge(s_to, 16)

        @block.gpsimd
        def _(pool):
            nc.gpsimd.memset(ones[:, :], 1.0)
            nc.gpsimd.memset(eps_col[:, :], EPS)
            nc.gpsimd.memset(ones3[:, :], 1.0)
            nc.gpsimd.iota(tidx[:, 2:3], [[0, 1]], base=0, channel_multiplier=J).then_inc(s_const, 1)
            pool.wait_ge(s_const, 1)
            nc.gpsimd.affine_select(out=ident[:, :], in_=ones[:, :], compare_op=ALU.is_equal, fill=0.0, base=0,
                                    pattern=[[1, P]], channel_multiplier=-1)
            nc.gpsimd.affine_select(out=below[:, :], in_=ones[:, :], compare_op=ALU.is_gt, fill=0.0, base=0,
                                    pattern=[[1, P]], channel_multiplier=-1)
            nc.gpsimd.affine_select(out=above[:, :], in_=ones[:, :], compare_op=ALU.is_gt, fill=0.0, base=0,
                                    pattern=[[-1, P]], channel_multiplier=1).then_inc(s_const, 1)

            pool.wait_ge(s_prep, FLAG)
            unordered = pool.value_load(flag_i[0:1, 0:1], min_val=0, max_val=1)
            with pool.If(unordered > 0):
                pool.dma_start(keys_i[:, 0:E], dst.partition_broadcast(P)).then_inc(s_key, 16)
                pool.wait_ge(s_rank, 1)
                last_row = pool.to_reg(EPAD - 1)
                with pool.Fori(0, J) as t:
                    nc.gpsimd.tensor_copy(stage_r[:, :], rank_i[:, bass.ds(t, 1)])
                    nc.gpsimd.tensor_copy(stage_e[:, :], rec[:, bass.ds(t * 4, 4)]).then_inc(s_stage, 1)
                    pool.wait_ge(s_stage, t + 1)
                    pool.reg_alu(last_row, last_row, EPAD - 1, ALU.min)
                    pool.indirect_dma_start(
                        out=sorted_dram, out_offset=bass.IndirectOffsetOnAxis(ap=stage_r[:, 0:1], axis=0),
                        in_=stage_e[:, :], in_offset=None, bounds_check=last_row, oob_is_err=False,
                    ).then_inc(s_row, 16)
                    pool.wait_ge(s_row, t * 16 + 16)
                pool.dma_start(rec[:, :], sorted_dram.rearrange("(p j) c -> p (j c)", j=J)).then_inc(s_back, 16)
                pool.wait_ge(s_back, 16)
            with pool.Else():
                pool.nop()

            pool.wait_ge(s_prep, INDICES)
            if_tail = dict(bounds_check=N - 1, oob_is_err=False)

            def gather(dest, rows, idx, s):
                pool.indirect_dma_start(out=dest, out_offset=None, in_=rows,
                                        in_offset=bass.IndirectOffsetOnAxis(ap=idx, axis=0),
                                        **(if_tail if rows is x else {})).then_inc(s, 16)

            def scatter(rows, idx, s):
                pool.indirect_dma_start(out=out, out_offset=bass.IndirectOffsetOnAxis(ap=idx, axis=0),
                                        in_=rows, in_offset=None, **if_tail).then_inc(s, 16)

            def gather_row(g, n):
                if n == 0 and g >= 4:
                    pool.wait_ge(s_gath[g % 4], 2 * G * 16 * (g // 4))
                c = g * G + n % G
                gather(slot(Group(g), n // G)[:, n % G, :], x, (gidx if n >= G else src_i)[:, c:c + 1], s_gath[g % 4])

            done = 0
            for g in range(NG):
                upto = (g + 1) * RING * 2 * G // NG
                for n in range(done, upto):
                    gather_row(n // (2 * G), n % (2 * G))
                done = upto
                nd["relu_v"].after(pool, Group(g))
                final(pool, nc.gpsimd, nd, Group(g), o[:, g % 4])
            for g in range(4):
                ed["h"].after(pool, Group(g), 1)
                for n in range(G):
                    gather_row(g + RING, n)
            refills = [(g, n) for g in range(RING, EG) for n in range(0 if g >= RING + 4 else G, 2 * G)]
            for i in range(4):
                pool.wait_ge(s_st[i], 16 * len(range(i, NG, 4)))
            refilled = 0
            for g in range(EG):
                if g == EG - 2:
                    for i in range(4):
                        pool.wait_ge(s_sums[i], 16 * len(range(i, EG, 4)))
                    gather(tail_f, sums_dram, tidx[:, 2:3], s_tf)
                final(pool, nc.gpsimd, ed, Group(g), o[:, g % 4])
                upto = min(len(refills), (g + 1) * REFILL)
                for row in refills[refilled:upto]:
                    gather_row(*row)
                refilled = upto
                pool.wait_ge(ed["final"].sem, g + 1)
                for k in range(G):
                    c = g * G + k
                    scatter(o[:, g % 4, k, :], sidx[:, c:c + 1], s_scat[g % 4])
                if g == TAIL_SLOT:
                    gather(tail_x, x, tidx[:, 0:1], s_tx)
            pool.wait_ge(tl["final"].sem, 1)
            scatter(tail_o, tidx[:, 1:2], s_to)
            pool.wait_ge(s_to, 16)

        @block.vector
        def _(dve):
            prep_n = [0]

            def link(ins):
                prep_n[0] += 1
                ins.then_inc(s_prep, 1)
                dve.wait_ge(s_prep, prep_n[0])

            nc.vector.memset(src_i[:, :], 0)
            nc.vector.memset(dst_i[:, :], NO_NODE)
            nc.vector.memset(w_f[:, :], 0.0).then_inc(s_memset, 1)
            nc.vector.memset(cont[:, :], 0.0)
            nc.vector.memset(mv[:, :, :, :], 1.0)
            link(nc.vector.memset(ones_j, 1.0))
            dve.wait_ge(s_e, 6 * 16)
            dve.wait_ge(s_const, 2)

            def node_step(s):
                g = s.back(4)
                fin, new = live(g, NG), live(s, NG)
                if fin:
                    gain(dve, nd, g, 0)
                r = s.back(6)
                if live(r, NG):
                    nd["beta"].after(dve, r)
                    b = r.at % 4
                    one_mark(nd["relu_v"], dve, r, nc.vector.tensor_scalar(
                        t_buf[:, b, G - 1, :], t_buf[:, b, G - 1, :], 0.0, gt[:, b, G - 1:G], ALU.max, ALU.mult))
                if new:
                    dve.wait_ge(s_x[s.at % XS], s.rounds(16, 16, XS))
                    L = nd["stats"]
                    row_stats(L, s, xload[:, s.at % XS, 0:1], 0)
                if fin:
                    gain(dve, nd, g, 1)
                if new:
                    row_stats(L, s, xload[:, s.at % XS, 1:2], 1)
                if fin:
                    gain(dve, nd, g, 2)
                if live(s.back(1), NG):
                    minus_mean(dve, nd, s.back(1), G)
                if new:
                    L.begin(dve, s)
                    L.mark(row_stats(L, s, xload[:, s.at % XS, 2:4], 2))
                if fin:
                    if beyond(g, 4):
                        dve.wait_ge(s_st[g.at % 4], g.rounds(16))
                    nd["rstd"].after(dve, s)
                    one_mark(nd["gamma"], dve, g, by_std(t_buf[:, g.at % 4], py[:, g.at % 2], s.at % 4, G, g_upd, G,
                                                         L.wait if new else None))
                elif new:
                    L.wait()
                if new:
                    aggregate(L, s, G)
                if fin:
                    nd["gain"].after(dve, g)
                    for k in range(G):
                        last = mix_row(g, k, hrow[:, g.at % 4], xload[:, g.at % XS], o[:, g.at % 4])
                    one_mark(nd["mix"], dve, g, last)
                    beta(dve, nd, g, t_buf[:, g.at % 4], be_upd)

            def border_columns():
                link(nc.vector.tensor_copy(dst_f, dst_i[:, :]))
                nc.vector.tensor_scalar(dbf, ones[:, :], dst_f[:, 0:1], None, ALU.mult)
                link(nc.vector.tensor_scalar(dbl, ones[:, :], dst_f[:, J - 1:J], None, ALU.mult))

            border_columns()
            assert prep_n[0] == BORDERS1, prep_n
            nc.vector.tensor_tensor(viol[:, 0:J - 1], dst_f[:, 0:J - 1], dst_f[:, 1:J], ALU.is_gt)
            link(nc.vector.memset(viol[:, J - 1:J], 0.0))
            link(nc.vector.reduce_sum(col[:, 0:1], viol, AX.X))
            dve.wait_ge(s_prep_pe, 1)
            link(nc.vector.scalar_tensor_tensor(scr, pm[:, 0, :], dst_f[:, J - 1:J], below[:, :],
                                                ALU.is_lt, ALU.mult, accum_out=col[:, 1:2]))
            link(nc.vector.tensor_tensor(col[:, 2:3], col[:, 0:1], col[:, 1:2], ALU.add))
            assert prep_n[0] == VIOLATIONS, prep_n
            dve.wait_ge(s_prep_pe, 2)
            link(nc.vector.tensor_scalar(flag_i[0:1, 0:1], pm[0:1, 2, 0:1], 1.0, None, ALU.min))
            assert prep_n[0] == FLAG, prep_n
            unordered = dve.value_load(flag_i[0:1, 0:1], min_val=0, max_val=1)
            with dve.If(unordered > 0):
                fall = [0]

                def flink(ins, n=None):
                    fall[0] += 1
                    ins.then_inc(s_fall, 1)
                    dve.wait_ge(s_fall, fall[0] if n is None else n)

                nc.vector.memset(keys[:, E:EPAD], float(NO_NODE))
                nc.vector.memset(rec[:, :], 0)
                dve.wait_ge(s_key, 16)
                flink(nc.vector.tensor_copy(keys[:, 0:E], keys_i[:, 0:E]))
                key_cols = keys[:, :].rearrange("p (q j) -> p q j", j=J)
                half = EPAD // 2
                with dve.Fori(0, J) as t:
                    d = dst_f[:, bass.ds(t, 1)]
                    for m in range(2):
                        nc.vector.tensor_scalar(smaller[:, m * half:(m + 1) * half], keys[:, m * half:(m + 1) * half], d, None,
                                                ALU.is_lt, ALU.add, accum_out=col[:, 4 + m:5 + m])
                    nc.vector.scalar_tensor_tensor(scr, key_cols[:, :, bass.ds(t, 1)].rearrange("p q a -> p (q a)"), d,
                                                   above[:, :], ALU.is_equal, ALU.mult,
                                                   accum_out=col[:, 6:7]).then_inc(s_fall, 1)
                    dve.wait_ge(s_fall, t * 3 + 2)
                    nc.vector.tensor_scalar(key_cols[:, :, bass.ds(t, 1)], key_cols[:, :, bass.ds(t, 1)], 0.5, None,
                                            ALU.subtract)
                    nc.vector.tensor_tensor(col[:, 7:8], col[:, 4:5], col[:, 5:6], ALU.add).then_inc(s_fall, 1)
                    dve.wait_ge(s_fall, t * 3 + 3)
                    nc.vector.tensor_tensor(rank_i[:, bass.ds(t, 1)], col[:, 7:8], col[:, 6:7],
                                            ALU.add).then_inc(s_fall, 1)
                    dve.wait_ge(s_fall, t * 3 + 4)
                rec_v = rec[:, :].rearrange("p (j c) -> p j c", c=4)
                nc.vector.tensor_copy(rec_v[:, :, 0], src_i[:, :])
                nc.vector.tensor_copy(rec_v[:, :, 1], dst_i[:, :])
                nc.vector.tensor_copy(rec_v[:, :, 2].bitcast(f32), w_f[:, :]).then_inc(s_rank, 1)
                dve.wait_ge(s_back, 16)
                nc.vector.tensor_copy(src_i[:, :], rec_v[:, :, 0])
                nc.vector.tensor_copy(dst_i[:, :], rec_v[:, :, 1])
                nc.vector.tensor_copy(w_f[:, :], rec_v[:, :, 2].bitcast(f32)).then_inc(s_rank, 1)
                dve.wait_ge(s_rank, 2)
            with dve.Else():
                nc.vector.memset(col[:, 8:9], 0.0)

            border_columns()
            assert prep_n[0] == BORDERS2, prep_n
            link(nc.vector.tensor_tensor(cont[:, 1:J], dst_f[:, 1:J], dst_f[:, 0:J - 1], ALU.is_equal))
            nc.vector.tensor_tensor_scan(run_f, cont[:, 0:J], ones_j, 0.0, ALU.mult, ALU.add)
            nc.vector.tensor_tensor_scan(run_b[:, ::-1], cont[:, 1:J + 1][:, ::-1], ones_j, 0.0, ALU.mult, ALU.add)
            nc.vector.tensor_scalar(is_first, dst_f, dst_f[:, 0:1], None, ALU.is_equal)
            link(nc.vector.tensor_scalar(is_last, dst_f, dst_f[:, J - 1:J], None, ALU.is_equal))
            nc.vector.tensor_copy(col[:, 9:10], run_f[:, J - 1:J])
            link(nc.vector.reduce_sum(col[:, 10:11], is_first, AX.X))
            dve.wait_ge(s_prep_pe, 3)
            nc.vector.scalar_tensor_tensor(carry_m[:, :], pm[:, 0, :], dst_f[:, J - 1:J], below[:, :],
                                           ALU.is_equal, ALU.mult)
            link(nc.vector.scalar_tensor_tensor(m2, pm[:, 1, :], dst_f[:, 0:1], above[:, :],
                                                ALU.is_equal, ALU.mult))
            assert prep_n[0] == MATRICES, prep_n
            link(nc.vector.tensor_tensor(cnt, run_f, run_b, ALU.add))
            dve.wait_ge(s_prep_pe, 4)
            link(nc.vector.tensor_copy(col[:, 12:14], pm[:, 2, 0:2]))

            node_step(Group(0))
            node_step(Group(1))

            dve.wait_ge(s_w, 10 * 16)
            nc.vector.reduce_sum(bias_sum[0:1, 0:2], bias[0:1, 0, 0:2 * H].rearrange("p (a h) -> p a h", a=2), AX.X)
            link(nc.vector.reduce_sum(wmean[:, :], w_all[:, :, :], AX.X))
            nc.vector.tensor_scalar(bias_sum[0:1, :], bias_sum[0:1, :], 1.0 / H, None, ALU.mult)
            link(nc.vector.tensor_scalar(wmean[:, :], wmean[:, :], 1.0 / H, None, ALU.mult))
            for a in range(4):
                nc.vector.tensor_scalar(w_all[:, a, :], w_all[:, a, :], wmean[:, a:a + 1], None, ALU.subtract)
            for a in range(2):
                last = nc.vector.tensor_scalar(bias[0:1, 0, a * H:(a + 1) * H], bias[0:1, 0, a * H:(a + 1) * H],
                                               bias_sum[0:1, a:a + 1], None, ALU.subtract)
            link(last)
            nc.vector.tensor_copy(w_u1[:, 0:H], w_all[:, 2, :])
            link(nc.vector.tensor_copy(bias_b[0:1, 0, :], bias[0:1, 0, :]))
            link(nc.vector.tensor_tensor(bias[0:1, 1, :], bias[0:1, 0, :], bias_b[0:1, 0, :], ALU.subtract))
            link(nc.vector.tensor_copy(bias_b[0:1, 1, :], bias[0:1, 1, :]))
            link(nc.vector.tensor_tensor(bias[0:1, 2, :], bias[0:1, 1, :], bias_b[0:1, 1, :], ALU.subtract))
            nc.vector.tensor_copy(bias_b[0:1, 2, :], bias[0:1, 2, :]).then_inc(s_bsplit, 1)
            dve.wait_ge(s_bsplit, 1)
            assert prep_n[0] == WEIGHTS, prep_n

            node_step(Group(2))

            before_n, after_n = col[:, 12:13], col[:, 13:14]
            link(nc.vector.scalar_tensor_tensor(cnt, is_first, before_n, cnt, ALU.mult, ALU.add))
            link(nc.vector.scalar_tensor_tensor(cnt, is_last, after_n, cnt, ALU.mult, ALU.add))
            link(nc.vector.tensor_scalar(cnt, cnt, -1.0, None, ALU.add))
            nc.vector.tensor_scalar(col[:, 14:15], before_n, 0.0, None, ALU.is_gt)
            nc.vector.tensor_scalar(col[:, 15:16], after_n, 0.0, None, ALU.is_gt)
            link(nc.vector.reciprocal(cnt, cnt))
            node_step(Group(3))
            nc.vector.tensor_scalar(col[:, 16:17], col[:, 10:11], float(J), None, ALU.is_equal)
            nc.vector.tensor_tensor(cnt, cnt, w_f[:, :], ALU.mult)
            nc.vector.tensor_scalar(ok[:, 0:J - 1], cont[:, 1:J], -1.0, 1.0, ALU.mult, ALU.add)
            nc.vector.tensor_scalar(ok[:, J - 1:J], col[:, 15:16], -1.0, 1.0, ALU.mult, ALU.add)
            link(nc.vector.tensor_scalar(is_first, is_first, col[:, 14:15], None, ALU.mult))
            nc.vector.tensor_tensor(col[:, 17:18], col[:, 16:17], col[:, 15:16], ALU.mult)
            link(nc.vector.tensor_scalar(is_first, is_first, -1.0, 1.0, ALU.mult, ALU.add))
            nc.vector.tensor_scalar(col[:, 18:19], col[:, 17:18], -1.0, 1.0, ALU.mult, ALU.add)
            link(nc.vector.tensor_tensor(ok, ok, is_first, ALU.mult))
            nc.vector.tensor_tensor(col[:, 19:20], col[:, 18:19], col[:, 14:15], ALU.mult)
            link(nc.vector.scalar_tensor_tensor(ok, dst_f, float(N), ok, ALU.is_lt, ALU.mult))
            nc.vector.tensor_scalar(col[:, 20:21], col[:, 19:20], -FAR, FAR, ALU.mult, ALU.add)
            link(nc.vector.tensor_scalar(ok, ok, -FAR, FAR, ALU.mult, ALU.add))
            nc.vector.tensor_tensor(sidx[:, :], dst_f, ok, ALU.add)
            nc.vector.tensor_tensor(tidx[:, 1:2], dst_f[:, 0:1], col[:, 20:21], ALU.add)
            nc.vector.tensor_copy(tidx[:, 0:1], dst_f[:, 0:1])
            cw_v = cont_wb[:, :].rearrange("p (g a k) -> p g a k", a=2, k=G)
            nc.vector.tensor_copy(cw_v[:, :, 0, :], cont[:, 0:J].rearrange("p (g k) -> p g k", k=G))
            nc.vector.tensor_copy(cw_v[:, :, 1, :], cnt.rearrange("p (g k) -> p g k", k=G))
            nc.vector.scalar_tensor_tensor(tidx[:, 2:3], col[:, 10:11], -1.0, tidx[:, 2:3], ALU.add, ALU.add)
            link(nc.vector.tensor_scalar(gidx[:, :], dst_f, float(N - 1), None, ALU.min))
            assert prep_n[0] == INDICES, prep_n

            nc.vector.memset(acc[:, 3, G - 1, :], 0.0).then_inc(s_bsplit, 1)
            dve.wait_ge(s_bsplit, 2)

            def edge_step(s):
                g, m = s.back(6), s.back(4)
                fin, new, summing = live(g, EG), live(s, EG), live(m, EG)
                q = s.back(3)
                if live(q, EG):
                    c = q.times(2 * G)
                    own = cont_wb[:, c:c + 2 * G] if q.turn is None else cont_wb[:, bass.ds(dve.snap(c), 2 * G)]
                    one_mark(ed["cw"], dve, q, nc.vector.tensor_copy(cw[:, q.at % 4, :], own))
                if fin:
                    gain(dve, ed, g, 0)
                if new:
                    dve.wait_ge(s_gath[s.at % 4], s.rounds(2 * G * 16, 2 * G * 16))
                    at = slot_base(dve, s)
                    L = ed["stats"]
                    row_stats(L, s, slot(s, 0, at)[:, 0:2], 0)
                if fin:
                    gain(dve, ed, g, 1)
                if new:
                    row_stats(L, s, slot(s, 0, at)[:, 2:4], 2)
                if fin:
                    gain(dve, ed, g, 2)
                if live(s.back(1), EG):
                    minus_mean(dve, ed, s.back(1), 2 * G, -0.5)
                q = s.back(3)
                if live(q, EG):
                    if beyond(q, 4):
                        dve.wait_ge(s_sums[q.at % 4], q.rounds(16))
                    ed["rstd"].after(dve, s)
                    one_mark(ed["gamma_m"], dve, q, by_std(acc[:, q.at % 4], pm, s.at % 4, 2 * G, g_msg))
                if new:
                    L.begin(dve, s)
                    L.mark(row_stats(L, s, slot(s, 1, at), G))
                if fin:
                    if beyond(g, 4):
                        dve.wait_ge(s_scat[g.at % 4], g.rounds(16 * G))
                    else:
                        dve.wait_ge(s_st[g.at], 16 * len(range(g.at, NG, 4)))
                    ed["gain"].after(dve, g)
                    fat = slot_base(dve, g)
                if summing:
                    ed["msgw"].after(dve, m)
                    before = acc[:, (m.at - 1) % 4, G - 1, :]
                    S = ed["sum"]
                    S.begin(dve, m)
                for k in range(G):
                    if summing:
                        if k:
                            S.wait()
                        S.mark(nc.vector.scalar_tensor_tensor(acc[:, m.at % 4, k, :], before, cw[:, m.at % 4, k:k + 1],
                                                              acc[:, m.at % 4, k, :], ALU.mult, ALU.add))
                        before = acc[:, m.at % 4, k, :]
                    if fin:
                        last = mix_row(g, k, h_dst[:, (g.at + NG) % XS], slot(g, 1, fat), o[:, g.at % 4])
                    if new and k in (0, 2):
                        L.wait()
                        moment(L, s, 2 * G, k // 2)
                if fin:
                    one_mark(ed["mix"], dve, g, last)
                if new:
                    L.wait()
                    moment(L, s, 2 * G, 2)
                if fin:
                    ed["rstd"].after(dve, s)
                    one_mark(ed["gamma"], dve, g, by_std(t_buf[:, g.at % 4], py[:, g.at % 2], s.at % 4, 3 * G, g_upd))
                if live(q, EG):
                    beta(dve, ed, q, acc[:, q.at % 4], be_msg, G, "beta_m", "gamma_m")
                if fin:
                    beta(dve, ed, g, t_buf[:, g.at % 4], be_upd)
                if live(q, EG):
                    weights = cw[:, q.at % 4, G:2 * G]
                    ed["cw"].after(dve, q)
                    ed["beta_m"].after(dve, q)
                    one_mark(ed["msgw"], dve, q, nc.vector.scalar_tensor_tensor(
                        acc[:, q.at % 4], acc[:, q.at % 4], 0.0, weights.unsqueeze(2).to_broadcast([P, G, H]),
                        ALU.max, ALU.mult))

            run_steps(dve, node_step, NG, 6, 9, 8, first=4, beside=edge_step)
            z = Group(0)
            tx, th = tail_x.unsqueeze(1), tail_h.unsqueeze(1)

            def tail_step(s):
                L = tl["stats"]
                if s.at == 1:
                    dve.wait_ge(s_tx, 16)
                    L.begin(dve, z)
                    L.mark(nc.vector.bn_stats(tail_st[:, :], tail_x))
                elif s.at == 2:
                    L.wait()
                    L.mark(nc.vector.bn_aggr(tail_mv[:, 0, :], tail_st[:, :]))
                elif s.at == 4:
                    tl["rstd"].after(dve, z)
                    one_mark(tl["nb"], dve, z, nc.vector.scalar_tensor_tensor(
                        tail_nb[:, :], tail_mv[:, 0, 0:1], -1.0, tail_rs[:, 0:1], ALU.mult, ALU.mult))

            run_steps(dve, edge_step, EG, 7, 2 * EUN, EUN, first=6, beside=tail_step)

            tl["msg"].after(dve, z)
            dve.wait_ge(s_tf, 16)
            one_mark(tl["sum"], dve, z, nc.vector.tensor_tensor(tail_a, pm[:, 0, :], tail_f, ALU.add))
            for k in range(3):
                gain(dve, tl, z, k, 1)
            tl["gain"].after(dve, z)
            one_mark(tl["mix"], dve, z, mix_row(z, 0, th, tx, tail_o.unsqueeze(1)))
            ed["final"].after(dve, Group(EG - 1))
            dve.wait_ge(tl["rstd"].sem, 2)
            one_mark(tl["gamma"], dve, z, nc.vector.scalar_tensor_tensor(
                t_buf[:, 0, 0, :], py[:, 0, 0, 0:H], tail_rs[:, 1:2], g_upd[:, :], ALU.mult, ALU.mult))
            beta(dve, tl, z, t_buf[:, 0, 0:1], be_upd, 1)
            final(dve, nc.vector, tl, z, tail_o.unsqueeze(1), 1)

        @block.scalar
        def _(act):
            nc.scalar.preload_act_table_set("natural_log_exp_and_others")
            act.wait_ge(s_prep, BORDERS1)

            def evacuate(d, g, dest, source, func, stage, flip):
                d[flip].after(act, g)
                one_mark(d[stage], act, g, nc.scalar.activation(dest, source, func))

            def node_step(s):
                r = s.back(6)
                if live(r, NG):
                    gated_relu(act, nd, r, 1, done=False)
                if live(s.back(1), NG):
                    nd["stats"].after(act, s.back(1))
                if live(s.back(4), NG):
                    nd["post"].after(act, s.back(4))
                logs(act, nd, s, 2 * G)
                filling = not beyond(s, 4)
                if filling:
                    rstds(act, nd, s, 2 * G)
                g = s.back(2)
                if live(g, NG):
                    evacuate(nd, g, ht_dst[:, g.at % 4, :], pt[:, g.at % 2, :], ACT.Copy, "ht", "flip")
                if not filling:
                    rstds(act, nd, s, 2 * G)
                if live(r, NG):
                    gated_relu(act, nd, r, G - 1, first=1)
                g = s.back(1)
                if live(g, NG):
                    nd["nb"].after(act, g)
                    one_mark(nd["h"], act, g, h_rows(g, hrow[:, g.at % 4], xload[:, g.at % XS], 0))
                if live(s.back(3), NG):
                    post(act, nd, s.back(3), (s.at + 1) % 4, G)

            def edge_step(s):
                if live(s.back(1), EG):
                    ed["stats"].after(act, s.back(1))
                if live(s.back(6), EG):
                    ed["post"].after(act, s.back(6))
                if live(s.back(3), EG):
                    ed["square_m"].after(act, s.back(3))
                logs(act, ed, s, 4 * G, 1.0 / H)
                g = s.back(2)
                if live(g, EG):
                    ed["flip"].after(act, g)
                    nc.scalar.activation(ht_src[:, g.at % 2, :], pt[:, 0, :], ACT.Copy)
                rstds(act, ed, s, 4 * G)
                if live(g, EG):
                    one_mark(ed["ht"], act, g, nc.scalar.activation(ht_dst[:, (g.at + NG) % 4, :], pt[:, 1, :], ACT.Copy))
                if live(s.back(7), EG):
                    gated_relu(act, ed, s.back(7))
                if live(s.back(5), EG):
                    post(act, ed, s.back(5), (s.at + 1) % 4, 3 * G, G, 1.0)
                g = s.back(1)
                if live(g, EG):
                    ed["nb"].after(act, g)
                    at = slot_base(act, g)
                    H_ = ed["h"]
                    H_.begin(act, g)
                    H_.mark(h_rows(g, hrow[:, (g.at + NG) % 4], slot(g, 0, at), 0))
                if live(g, EG):
                    H_.mark(h_rows(g, h_dst[:, (g.at + NG) % XS], slot(g, 1, at), G))
                g = s.back(4)
                if live(g, EG):
                    evacuate(ed, g, at_[:, g.at % 2, :], pa[:, :], ACT.Copy, "at", "aflip")
                if live(s.back(2), EG):
                    ed["msg"].after(act, s.back(2))
                    one_mark(ed["square_m"], act, s.back(2), squares(pm, (s.at + 1) % 4, 2 * G, G, 1, 1.0))

            run_steps(act, node_step, NG, 6, 9, 8, beside=edge_step)
            z = Group(0)

            def tail_std(n):
                nc.scalar.activation(tail_ln[:, n:n + 1], tail_mv[:, n, 1:2], ACT.Ln, bias=eps_col[:, :]
                                     ).then_inc(tl["ln"].sem, 1)
                act.wait_ge(tl["ln"].sem, n + 1)
                nc.scalar.activation(tail_rs[:, n:n + 1], tail_ln[:, n:n + 1], ACT.Exp, scale=-0.5
                                     ).then_inc(tl["rstd"].sem, 1)

            def tail_step(s):
                if s.at == 3:
                    tl["stats"].after(act, z)
                    tail_std(0)
                elif s.at == 5:
                    tl["nb"].after(act, z)
                    one_mark(tl["h"], act, z, nc.scalar.activation(tail_h, tail_x, ACT.Relu, bias=tail_nb[:, :],
                                                                   scale=tail_rs[:, 0:1]))

            run_steps(act, edge_step, EG, 7, 2 * EUN, EUN, first=6, beside=tail_step)

            evacuate(tl, z, ht_dst[:, 0, 0:H], pt[:, 0, 0:H], ACT.Copy, "ht", "flip")
            evacuate(tl, z, at_[:, 1, 0:H], pa[:, 0:H], ACT.Copy, "at", "aflip")
            tl["upd"].after(act, z)
            nc.scalar.activation(junk[:, 0, 0, :], py[:, 0, 0, 0:H], ACT.Square, scale=float(H) ** -0.5,
                                 accum_out=tail_mv[:, 1, 1:2])
            one_mark(tl["post"], act, z, nc.scalar.activation(ge[:, 0, 0:1], py[:, 0, 0:1, H], ACT.Exp, scale=-1.0))
            tl["post"].after(act, z)
            tail_std(1)
            gated_relu(act, tl, z, 1)

        @block.tensor
        def _(pe):
            def flip(dest, rows):
                for k in range(rows.shape[1]):
                    last = nc.tensor.transpose(dest[:, k * H:(k + 1) * H], rows[:, k, :], ident[:, :])
                return last

            def put_bias(dest, lo, hi):
                n = dest.shape[1]
                nc.tensor.matmul(dest, ones3[:, :], bias3[:, lo:hi].unsqueeze(1).to_broadcast([3, n, hi - lo]),
                                 start=True, stop=False)

            def spread(dest, column_spread):
                return nc.tensor.matmul(dest, column_spread, ident[:, :], start=True, stop=True)

            pe.wait_ge(s_const, 2)
            pe.wait_ge(s_prep, BORDERS1)
            spread(pm[:, 0, :], dbf).then_inc(s_prep_pe, 1)
            pe.wait_ge(s_prep, VIOLATIONS)
            nc.tensor.matmul(pm[0:1, 2, 0:1], col[:, 2:3], ones[:, 0:1], start=True, stop=True).then_inc(s_prep_pe, 1)
            pe.wait_ge(s_prep, BORDERS2)
            spread(pm[:, 0, :], dbf)
            spread(pm[:, 1, :], dbl).then_inc(s_prep_pe, 1)
            pe.wait_ge(s_prep, MATRICES)
            nc.tensor.matmul(pm[:, 2, 0:1], carry_m[:, :], col[:, 9:10], start=True, stop=True)
            nc.tensor.matmul(pm[:, 2, 1:2], m2, col[:, 10:11], start=True, stop=True).then_inc(s_prep_pe, 1)
            def node_step(s):
                g = s.back(1)
                if live(g, NG):
                    nd["h"].after(pe, g)
                    one_mark(nd["flip"], pe, g, flip(pt[:, g.at % 2, :], hrow[:, g.at % 4]))
                g = s.back(2)
                if live(g, NG):
                    nd["ht"].after(pe, g)
                    if beyond(g, 2):
                        nd["gamma"].after(pe, g.back(2))
                    for k in range(0, G, 2):
                        put_bias(py[:, g.at % 2, k:k + 2, 0:H + 1], H, 2 * H + 1)
                    for k in range(G):
                        last = nc.tensor.matmul(py[:, g.at % 2, k, 0:H + 1], ht_dst[:, g.at % 4, k * H:(k + 1) * H],
                                                w_u1[:, :], start=False, stop=k % 2 == 1)
                    one_mark(nd["upd"], pe, g, last)

            def edge_step(s):
                g = s.back(2)
                if live(g, EG):
                    ed["ht"].after(pe, g)
                    if beyond(g, 1):
                        ed["gamma_m"].after(pe, g.back(1))
                    put_bias(pm[:, :, :], 0, H)
                    for k in range(G):
                        nc.tensor.matmul(pm[:, k, :], ht_src[:, g.at % 2, k * H:(k + 1) * H], w_all[:, 0, :],
                                         start=False, stop=False)
                        last = nc.tensor.matmul(pm[:, k, :], ht_dst[:, (g.at + NG) % 4, k * H:(k + 1) * H], w_all[:, 1, :],
                                                start=False, stop=k == G - 1)
                    one_mark(ed["msg"], pe, g, last)
                g = s.back(4)
                if live(g, EG):
                    ed["sum"].after(pe, g)
                    one_mark(ed["aflip"], pe, g, flip(pa[:, :], acc[:, g.at % 4]))
                g = s.back(1)
                if live(g, EG):
                    ed["h"].after(pe, g)
                    flip(pt[:, 0, :], hrow[:, (g.at + NG) % 4])
                    one_mark(ed["flip"], pe, g, flip(pt[:, 1, :], h_dst[:, (g.at + NG) % XS]))
                g = s.back(4)
                if live(g, EG):
                    if beyond(g, 2):
                        ed["gamma"].after(pe, g.back(2))
                    else:
                        nd["gamma"].after(pe, Group(NG - 1))
                    ed["at"].after(pe, g)
                    for k in range(0, G, 2):
                        put_bias(py[:, g.at % 2, k:k + 2, 0:H + 1], H, 2 * H + 1)
                    for k in range(G):
                        nc.tensor.matmul(py[:, g.at % 2, k, 0:H], at_[:, g.at % 2, k * H:(k + 1) * H], w_all[:, 3, :],
                                         start=False, stop=False)
                        last = nc.tensor.matmul(py[:, g.at % 2, k, 0:H + 1], ht_dst[:, (g.at + NG) % 4, k * H:(k + 1) * H],
                                                w_u1[:, :], start=False, stop=k % 2 == 1)
                    one_mark(ed["upd"], pe, g, last)

            node_step(Group(0))
            node_step(Group(1))
            pe.wait_ge(s_b3, 16)
            pe.wait_ge(s_prep, WEIGHTS)
            run_steps(pe, node_step, NG, 2, 9, 8, first=2, beside=edge_step)
            run_steps(pe, edge_step, EG, 4, 2 * EUN, EUN, first=2)

            z = Group(0)
            nc.tensor.matmul(pm[:, 0, :], carry_m[:, :], acc[:, (EG - 1) % 4, G - 1, :], start=True, stop=True
                             ).then_inc(tl["msg"].sem, 1)
            tl["h"].after(pe, z)
            nc.tensor.transpose(pt[:, 0, 0:H], tail_h, ident[:, :]).then_inc(tl["flip"].sem, 1)
            pe.wait_ge(tl["sum"].sem, 1)
            nc.tensor.transpose(pa[:, 0:H], tail_a, ident[:, :]).then_inc(tl["aflip"].sem, 1)
            tl["ht"].after(pe, z)
            tl["at"].after(pe, z)
            put_bias(py[:, 0, 0:1, 0:H + 1], H, 2 * H + 1)
            nc.tensor.matmul(py[:, 0, 0, 0:H], at_[:, 1, 0:H], w_all[:, 3, :], start=False, stop=False)
            nc.tensor.matmul(py[:, 0, 0, 0:H + 1], ht_dst[:, 0, 0:H], w_u1[:, :], start=False, stop=True
                             ).then_inc(tl["upd"].sem, 1)


INPUTS = ["x", "src", "dst", "edge_weight"] + ["L0_gnn_" + n for n in (
    "msg_w", "msg_b", "msg_g", "msg_beta", "upd_w", "upd_b", "upd_g", "upd_beta", "gate_w", "gate_b")]


def kernel(**inputs):
    import numpy as np
    import concourse.bacc as bacc
    from concourse.bass_utils import run_bass_kernel_spmd

    nc = bacc.Bacc("TRN2", target_bir_lowering=False, num_devices=1)
    arrays, args = {}, []
    for name in INPUTS:
        a = np.ascontiguousarray(inputs[name])
        arrays[f"in_{name}"] = a
        args.append(nc.dram_tensor(f"in_{name}", a.shape, mybir.dt.from_np(a.dtype), kind="ExternalInput").ap())
    out = nc.dram_tensor("out", (N, H), f32, kind="ExternalOutput").ap()
    build(nc, *args, out)
    r = run_bass_kernel_spmd(nc, [arrays], core_ids=[0])
    return r.results[0]["out"]
```
